# Optimizing a Trainium2 kernel written in Bass

```python
import numpy as np
import jax
import jax.numpy as jnp

def _softmax(x, axis=-1):
    return jax.nn.softmax(x, axis=axis)

def _gelu(x):
    return jax.nn.gelu(x, approximate=True)

def _silu(x):
    return jax.nn.silu(x)

def _sigmoid(x):
    return jax.nn.sigmoid(x)

def _layernorm(x, axis=-1, eps=1e-05):
    m = jnp.mean(x, axis=axis, keepdims=True)
    v = jnp.var(x, axis=axis, keepdims=True)
    return (x - m) / jnp.sqrt(v + eps)

def _scatter_add(tgt, idx, src, axis=0):
    return tgt.at[idx].add(src)

def _segment_sum(src, seg, n):
    return jax.ops.segment_sum(src, seg, n)
kernel_name = 'mk_adj_ffn_d1_adj_r2_aa1d55'

def setup_inputs(seed: int=0):
    np.random.seed(seed)
    _w = jnp.asarray

    def _rec_inputs():
        import jax
        import jax.numpy as jnp
        _gk = jax.random.key(seed)
        x = -0.0002928 + 1 * jax.random.normal(jax.random.fold_in(_gk, 1), (64, 128, 128), jnp.float32)
        _a = jax.random.bernoulli(jax.random.fold_in(_gk, 2), 0.015625, (128, 128))
        _a = jnp.logical_or(_a, jnp.swapaxes(_a, -1, -2))
        _a = jnp.logical_or(_a, jnp.eye(128, dtype=bool))
        _af = _a.astype(jnp.float32)
        _af = _af * jax.random.uniform(jax.random.fold_in(_gk, 3), (128, 128), jnp.float32, 0.05, 1)
        adj = _af
        return (x, adj)
    x, adj = _rec_inputs()

    def _L0_gnn_setup():
        import jax, jax.numpy as jnp
        import numpy as np
        N = 2048
        NFEAT, NHID, NCLASS = (128, 256, 128)
        B = 4

        def _slconv(x, adj, S, W):
            support = jnp.einsum('bnf,fh->bnh', x, W)
            weighting = adj * S
            return jnp.einsum('nm,bmh->bnh', weighting, support)
        key = jax.random.key(seed)
        ks = jax.random.split(key, 6)
        x = jax.random.normal(ks[0], (B, N, NFEAT), dtype=jnp.float32)
        adj = jax.random.uniform(ks[1], (N, N), dtype=jnp.float32)
        S = jnp.ones((N, N), dtype=jnp.float32)
        W1 = jax.random.normal(ks[2], (NFEAT, NHID), dtype=jnp.float32) / np.sqrt(NFEAT)
        W2 = jax.random.normal(ks[3], (NHID, 2 * NHID), dtype=jnp.float32) / np.sqrt(NHID)
        W3 = jax.random.normal(ks[4], (2 * NHID, NCLASS), dtype=jnp.float32) / np.sqrt(2 * NHID)
        return {'x': x, 'adj': adj, 'S': S, 'W1': W1, 'W2': W2, 'W3': W3}
    _L0_gnn_all = _L0_gnn_setup()
    _L0_gnn_in = {k: v for k, v in _L0_gnn_all.items() if k in ('W1', 'W2', 'W3')}
    del _L0_gnn_all

    def _L0_ffn_setup():
        import jax, jax.numpy as jnp
        import numpy as np
        NUM_EXPERTS = 8
        TOP_K = 2
        B, S, D = (8, 4096, 128)

        def _moe(tokens, router_w, w1, b1, w2, b2):
            N = tokens.shape[0]
            E = router_w.shape[0]
            logits = tokens.astype(jnp.float32) @ router_w.astype(jnp.float32).T
            probs = jax.nn.softmax(logits, axis=-1)
            rw, re = jax.lax.top_k(probs, TOP_K)
            if TOP_K > 1:
                rw = rw / jnp.maximum(rw.sum(-1, keepdims=True), 1e-12)
            rw = rw.astype(tokens.dtype)
            combine = jnp.zeros((N, E), tokens.dtype).at[jnp.arange(N)[:, None], re].set(rw)
            out = tokens
            for e in range(E):
                h = jax.nn.gelu(tokens @ w1[e] + b1[e], approximate=False)
                y = h @ w2[e] + b2[e]
                out = out + combine[:, e:e + 1] * y
            return out
        key = jax.random.key(seed)
        ks = jax.random.split(key, 4)
        scale = 1.0 / np.sqrt(D).astype(np.float32)
        return {'input_embeddings': jax.random.normal(ks[0], (B, S, D), jnp.float32), 'router_w': jax.random.normal(ks[1], (NUM_EXPERTS, D), jnp.float32) * scale, 'w1': jax.random.normal(ks[2], (NUM_EXPERTS, D, D), jnp.float32) * scale, 'b1': jnp.zeros((NUM_EXPERTS, D), jnp.float32), 'w2': jax.random.normal(ks[3], (NUM_EXPERTS, D, D), jnp.float32) * scale, 'b2': jnp.zeros((NUM_EXPERTS, D), jnp.float32)}
    _L0_ffn_all = _L0_ffn_setup()
    _L0_ffn_in = {k: v for k, v in _L0_ffn_all.items() if k in ('router_w', 'w1', 'b1', 'w2', 'b2')}
    del _L0_ffn_all
    return {'x': x, 'adj': adj, 'L0_gnn_W1': _L0_gnn_in['W1'], 'L0_gnn_W2': _L0_gnn_in['W2'], 'L0_gnn_W3': _L0_gnn_in['W3'], 'L0_ffn_router_w': _L0_ffn_in['router_w'], 'L0_ffn_w1': _L0_ffn_in['w1'], 'L0_ffn_b1': _L0_ffn_in['b1'], 'L0_ffn_w2': _L0_ffn_in['w2'], 'L0_ffn_b2': _L0_ffn_in['b2']}

def reference(x, adj, L0_gnn_W1, L0_gnn_W2, L0_gnn_W3, L0_ffn_router_w, L0_ffn_w1, L0_ffn_b1, L0_ffn_w2, L0_ffn_b2):
    import jax
    import jax.numpy as jnp

    def _L0_gnn_ref(x, adj, S, W1, W2, W3):
        import jax, jax.numpy as jnp
        import numpy as np
        N = 2048
        NFEAT, NHID, NCLASS = (128, 256, 128)
        B = 4

        def _slconv(x, adj, S, W):
            support = jnp.einsum('bnf,fh->bnh', x, W)
            weighting = adj * S
            return jnp.einsum('nm,bmh->bnh', weighting, support)
        h = jax.nn.relu(_slconv(x, adj, S, W1))
        h = jax.nn.relu(_slconv(h, adj, S, W2))
        return _slconv(h, adj, S, W3)

    def _L0_ffn_ref(input_embeddings, router_w, w1, b1, w2, b2):
        import jax, jax.numpy as jnp
        import numpy as np
        NUM_EXPERTS = 8
        TOP_K = 2
        B, S, D = (8, 4096, 128)

        def _moe(tokens, router_w, w1, b1, w2, b2):
            N = tokens.shape[0]
            E = router_w.shape[0]
            logits = tokens.astype(jnp.float32) @ router_w.astype(jnp.float32).T
            probs = jax.nn.softmax(logits, axis=-1)
            rw, re = jax.lax.top_k(probs, TOP_K)
            if TOP_K > 1:
                rw = rw / jnp.maximum(rw.sum(-1, keepdims=True), 1e-12)
            rw = rw.astype(tokens.dtype)
            combine = jnp.zeros((N, E), tokens.dtype).at[jnp.arange(N)[:, None], re].set(rw)
            out = tokens
            for e in range(E):
                h = jax.nn.gelu(tokens @ w1[e] + b1[e], approximate=False)
                y = h @ w2[e] + b2[e]
                out = out + combine[:, e:e + 1] * y
            return out
        b, s, d = input_embeddings.shape
        tokens = input_embeddings.reshape(b * s, d)
        return _moe(tokens, router_w, w1, b1, w2, b2).reshape(b, s, d)
    x = x + _L0_gnn_ref(_layernorm(x, axis=-1), adj, adj, L0_gnn_W1, L0_gnn_W2, L0_gnn_W3)
    x = x + _L0_ffn_ref(_layernorm(x, axis=-1), L0_ffn_router_w, L0_ffn_w1, L0_ffn_b1, L0_ffn_w2, L0_ffn_b2)
    return x

_drawn_inputs = setup_inputs


def setup_inputs(seed=0):
    import zlib

    import numpy as np

    out = dict(_drawn_inputs(seed))
    spreads = {'L0_ffn_b1': (0.0, 0.464), 'L0_ffn_b2': (0.0, 0.333)}
    factors = {}
    for name, (base, spread) in spreads.items():
        noise = np.random.default_rng([zlib.crc32(name.encode()), seed]).standard_normal(out[name].shape)
        drawn = base * np.exp(spread * noise) if base else spread * noise
        out[name] = jnp.asarray(drawn.astype(out[name].dtype))
    for name, factor in factors.items():
        out[name] = (out[name] * factor).astype(out[name].dtype)
    return out
```

```python
import concourse.bass as bass
from concourse import mybir
from concourse.alu_op_type import AluOpType as ALU
from contextlib import ExitStack


def gnn_moe_kernel(
    nc: bass.Bass,
    x: bass.AP,
    adj_t: bass.AP,
    gnn_w1: bass.AP,
    gnn_w2: bass.AP,
    gnn_w3: bass.AP,
    router_t: bass.AP,
    ffn_w1: bass.AP,
    ffn_b1_t: bass.AP,
    ffn_w2: bass.AP,
    ffn_b2: bass.AP,
    out: bass.AP,
):
    f32 = mybir.dt.float32
    f32r = mybir.dt.float32r
    u32 = mybir.dt.uint32
    ACT = mybir.ActivationFunctionType
    AX = mybir.AxisListType.X

    GROUPS, P, GF = x.shape
    F = gnn_w1.shape[0]
    B = GF // F
    T = B * P
    H1 = gnn_w1.shape[1]
    H2 = gnn_w2.shape[1]
    C1 = H1 // P
    C2 = H2 // P
    E = ffn_w1.shape[1]
    TOP = 2
    BANK = 512
    BN = 6
    EPS = 1e-5
    GUARD = 1e-12
    DONE = 16
    HID_BUFS = 2
    GATED_BUFS = 4
    LOOP_FROM, LOOP_TO = 4, GROUPS - 2

    ctx = ExitStack()
    with ctx:
        def sb(name, shape, dt=f32):
            return ctx.enter_context(nc.sbuf_tensor(name, shape, dt))

        def pb(name):
            return ctx.enter_context(nc.psum_tensor(name, [P, BANK], f32))

        def sem(name):
            return ctx.enter_context(nc.semaphore(name))

        ident = sb("ident", [P, P])
        expert_id = sb("expert_id", [P, E])
        neg_half = sb("neg_half", [P, B])
        eps = sb("eps", [P, B])
        euler = sb("euler", [P, B * E])
        adj_sb = sb("adj_sb", [P, P])
        a_t = sb("a_t", [P, P])
        w1g = sb("w1g", [P, H1])
        w2_raw = sb("w2_raw", [P, C1, H2])
        w2_hi = sb("w2_hi", [P, C1, H2], f32r)
        w2_lo = sb("w2_lo", [P, C1, H2], f32r)
        w3g = sb("w3g", [P, C2, F])
        up_raw = sb("up_raw", [P, E, P])
        up_hi = sb("up_hi", [P, E, P], f32r)
        up_lo = sb("up_lo", [P, E, P], f32r)
        down = sb("down", [P, E, F])
        b1_sb = sb("b1_sb", [P, E])
        b2_sb = sb("b2_sb", [E, F])
        router_raw = sb("router_raw", [P, E])
        router = sb("router", [P, 2, E], f32r)

        x_sb = [sb(f"x_sb{i}", [P, B, F]) for i in range(2)]
        xhat1 = sb("xhat1", [P, B, F])
        stats1 = sb("stats1", [P, B, BN])
        moments1 = sb("moments1", [P, B, 2])
        var1 = sb("var1", [P, B])
        rstd1 = sb("rstd1", [P, B])
        ax_t = sb("ax_t", [P, T])
        h1 = sb("h1", [P, B, H1])
        ah_hi = sb("ah_hi", [P, C1, T], f32r)
        ah_lo = sb("ah_lo", [P, C1, T], f32r)
        h2_t = sb("h2_t", [P, C2, T])
        s3 = sb("s3", [P, B, F])
        x1 = sb("x1", [P, B, F])
        xhat2 = sb("xhat2", [P, B, F])
        stats2 = sb("stats2", [P, B, BN])
        moments2 = sb("moments2", [P, B, 2])
        var2 = sb("var2", [P, B])
        rstd2 = sb("rstd2", [P, B])
        base = [sb(f"base{i}", [P, B, F]) for i in range(2)]
        xt_hi = [sb(f"xt_hi{i}", [P, T], f32r) for i in range(2)]
        xt_lo = [sb(f"xt_lo{i}", [P, T], f32r) for i in range(2)]
        logits = sb("logits", [P, B, E])
        top_logit = sb("top_logit", [P, B])
        shifted = sb("shifted", [P, B, E])
        exps = sb("exps", [P, B, E])
        exp_sum = sb("exp_sum", [P, B])
        exp_inv = sb("exp_inv", [P, B])
        probs = sb("probs", [P, B, E])
        best = sb("best", [P, B, 8])
        best_at = sb("best_at", [P, B, 8], u32)
        best_id = sb("best_id", [P, B, TOP])
        pair_sum = sb("pair_sum", [P, B])
        pair_inv = sb("pair_inv", [P, B])
        pair_w = sb("pair_w", [P, B, TOP])
        chosen = sb("chosen", [P, B, TOP, E])
        weighed = sb("weighed", [P, B, TOP, E])
        combine = sb("combine", [P, B, E])
        ct_sb = sb("ct_sb", [E, T])
        gate = [sb(f"gate{i}", [P, E, T]) for i in range(2)]
        hid = [sb(f"hid{i}", [P, T]) for i in range(HID_BUFS)]
        gated = [sb(f"gated{i}", [P, T]) for i in range(GATED_BUFS)]
        yt_sb = sb("yt_sb", [P, T])
        out_sb = [sb(f"out_sb{i}", [P, B, F]) for i in range(2)]
        ct_dram = nc.dram_tensor("ct_dram", [GROUPS, E, T], f32, kind="Internal").ap()

        chain_ps = pb("chain_ps")
        pair_ps = [pb(f"pair_ps{i}") for i in range(2)]
        y_ps = pb("y_ps")
        route_ps = pb("route_ps")
        hid_ps = [pb(f"hid_ps{i}") for i in range(2)]
        yt_ps = pb("yt_ps")

        graph_loaded = sem("graph_loaded")
        w1_loaded = sem("w1_loaded")
        w2_loaded = sem("w2_loaded")
        w3_loaded = sem("w3_loaded")
        ffn_loaded = sem("ffn_loaded")
        x_loaded = [sem(f"x_loaded{i}") for i in range(2)]
        ct_stored = sem("ct_stored")
        gate_loaded = [sem(f"gate_loaded{i}") for i in range(2)]
        out_stored = [sem(f"out_stored{i}") for i in range(2)]
        ident_zero = sem("ident_zero")
        consts_ready = sem("consts_ready")
        ids_int = sem("ids_int")
        a_ready = sem("a_ready")
        w2_split_hi = sem("w2_split_hi")
        w2_split = sem("w2_split")
        ffn_split_hi = sem("ffn_split_hi")
        ffn_split = sem("ffn_split")
        stats1_done = sem("stats1_done")
        moments1_done = sem("moments1_done")
        var1_done = sem("var1_done")
        rstd1_done = sem("rstd1_done")
        xhat1_done = sem("xhat1_done")
        ax_product = sem("ax_product")
        ax_ready = sem("ax_ready")
        h1_product = sem("h1_product")
        h1_ready = sem("h1_ready")
        ah_product = sem("ah_product")
        ah_hi_ready = sem("ah_hi_ready")
        ah_lo_ready = sem("ah_lo_ready")
        h2_product = sem("h2_product")
        h2_ready = sem("h2_ready")
        s3_product = sem("s3_product")
        s3_ready = sem("s3_ready")
        as3_product = sem("as3_product")
        x1_done = sem("x1_done")
        stats2_done = sem("stats2_done")
        moments2_done = sem("moments2_done")
        var2_done = sem("var2_done")
        rstd2_done = sem("rstd2_done")
        xhat2_done = sem("xhat2_done")
        base_done = sem("base_done")
        xt_product = sem("xt_product")
        xt_hi_ready = sem("xt_hi_ready")
        xt_lo_ready = sem("xt_lo_ready")
        logits_product = sem("logits_product")
        softmax_link = sem("softmax_link")
        shifted_done = sem("shifted_done")
        exps_done = sem("exps_done")
        combine_done = sem("combine_done")
        ct_product = sem("ct_product")
        ct_ready = sem("ct_ready")
        hid_product = sem("hid_product")
        hid_ready = sem("hid_ready")
        gated_ready = sem("gated_ready")
        down_done = sem("down_done")
        yt_ready = sem("yt_ready")
        y_product = sem("y_product")
        out_ready = sem("out_ready")

        SOFTMAX_LINKS = 12

        def run_steps(eng, step):
            step(0, 0, graph=True, norm_next=True, select=False, experts=False)
            step(1, 1, graph=True, norm_next=True, select=True, experts=False)
            step(2, 0, graph=True, norm_next=True, select=True, experts=True)
            step(3, 1, graph=True, norm_next=True, select=True, experts=True)
            with eng.Fori(LOOP_FROM, LOOP_TO, 2) as s:
                for parity in range(2):
                    step(s + parity, parity, graph=True, norm_next=True, select=True, experts=True)
            step(LOOP_TO, 0, graph=True, norm_next=True, select=True, experts=True)
            step(LOOP_TO + 1, 1, graph=True, norm_next=False, select=True, experts=True)
            step(GROUPS, 0, graph=False, norm_next=False, select=True, experts=True)
            step(GROUPS + 1, 1, graph=False, norm_next=False, select=False, experts=True)

        def landed(group, parity, dmas=1):
            return (group - parity) * (DONE * dmas // 2) + DONE * dmas

        block = ctx.enter_context(nc.Block())

        @block.sync
        def _(sp):
            sp.dma_start(x_sb[0][:], x[0].rearrange("p (b f) -> p b f", b=B)).then_inc(x_loaded[0], DONE)
            sp.dma_start(adj_sb[:], adj_t).then_inc(graph_loaded, DONE)
            sp.dma_start(w1g[:], gnn_w1).then_inc(w1_loaded, DONE)
            sp.dma_start(w2_raw[:], gnn_w2.rearrange("(c p) h -> p c h", p=P)).then_inc(w2_loaded, DONE)
            sp.dma_start(w3g[:], gnn_w3.rearrange("(c p) f -> p c f", p=P)).then_inc(w3_loaded, DONE)
            sp.dma_start(router_raw[:], router_t).then_inc(ffn_loaded, DONE)
            sp.dma_start(up_raw[:], ffn_w1).then_inc(ffn_loaded, DONE)
            sp.dma_start(down[:], ffn_w2).then_inc(ffn_loaded, DONE)
            sp.dma_start(b1_sb[:], ffn_b1_t).then_inc(ffn_loaded, DONE)
            sp.dma_start(b2_sb[:], ffn_b2).then_inc(ffn_loaded, DONE)

            def step(s, parity, graph, norm_next, select, experts):
                c, m = s - 1, s - 2
                if norm_next:
                    x_from = x[bass.ds(s + 1, 1)].rearrange("o p (b f) -> (o p) b f", b=B)
                    if not (isinstance(s, int) and s == 0):
                        sp.wait_ge(x1_done, s)
                    sp.dma_start(x_sb[1 - parity][:], x_from).then_inc(x_loaded[1 - parity], DONE)
                if select:
                    ct_to = ct_dram[bass.ds(c, 1)].rearrange("o e t -> (o e) t")
                    gate_from = (ct_dram[bass.ds(c, 1)].rearrange("o e t -> o (e t)").partition_broadcast(P)
                                 .rearrange("p o (e t) -> p (o e) t", e=E))
                    if not (isinstance(s, int) and s < 3):
                        sp.wait_ge(yt_ready, c - 1)
                    sp.wait_ge(ct_ready, c + 1)
                    sp.dma_start(ct_to, ct_sb[:]).then_inc(ct_stored, DONE)
                    sp.wait_ge(ct_stored, (c + 1) * DONE)
                    sp.dma_start(gate[1 - parity][:], gate_from).then_inc(gate_loaded[1 - parity], DONE)
                if experts:
                    out_to = out[bass.ds(m, 1)].rearrange("o p (b f) -> (o p) b f", b=B)
                    sp.wait_ge(out_ready, m + 1)
                    sp.dma_start(out_to, out_sb[parity][:]).then_inc(out_stored[parity], DONE)

            run_steps(sp, step)
            for parity in range(2):
                sp.wait_ge(out_stored[parity], GROUPS // 2 * DONE)

        @block.gpsimd
        def _(pool):
            nc.gpsimd.memset(ident[:], 0.0).then_inc(ident_zero, 1)
            nc.gpsimd.memset(neg_half[:], -0.5)
            nc.gpsimd.memset(eps[:], EPS)
            nc.gpsimd.memset(euler[:], 2.718281828459045)
            nc.gpsimd.iota(best_at[:, 0, 0:E], pattern=[[1, E]], base=0, channel_multiplier=0).then_inc(ids_int, 1)
            pool.wait_ge(ids_int, 1)
            nc.gpsimd.tensor_copy(expert_id[:], best_at[:, 0, 0:E])
            pool.wait_ge(ident_zero, 1)
            nc.gpsimd.affine_select(out=ident[:], in_=ident[:], compare_op=ALU.not_equal, fill=1.0, base=0,
                                    pattern=[[-1, P]], channel_multiplier=1).then_inc(consts_ready, 1)

            def root(group, moments_done, moments, var, var_done, rstd, rstd_done):
                pool.wait_ge(moments_done, group + 1)
                nc.gpsimd.tensor_tensor(var[:], moments[:, :, 1], eps[:], ALU.add).then_inc(var_done, 1)
                pool.wait_ge(var_done, group + 1)
                nc.gpsimd.tensor_tensor(rstd[:], var[:], neg_half[:], ALU.pow).then_inc(rstd_done, 1)

            def step(s, parity, graph, norm_next, select, experts):
                if select:
                    pool.wait_ge(shifted_done, s)
                    nc.gpsimd.tensor_tensor(exps[:].rearrange("p b e -> p (b e)"), euler[:],
                                            shifted[:].rearrange("p b e -> p (b e)"), ALU.pow).then_inc(exps_done, 1)
                if norm_next:
                    root(s + 1, moments1_done, moments1, var1, var1_done, rstd1, rstd1_done)
                if graph:
                    root(s, moments2_done, moments2, var2, var2_done, rstd2, rstd2_done)
                    pool.wait_ge(xhat2_done, s + 1)
                    if experts:
                        pool.wait_ge(out_ready, s - 1)
                    nc.gpsimd.tensor_tensor(base[parity][:], x1[:], xhat2[:], ALU.add).then_inc(base_done, 1)

            pool.wait_ge(consts_ready, 1)
            root(0, moments1_done, moments1, var1, var1_done, rstd1, rstd1_done)
            run_steps(pool, step)

        @block.vector
        def _(dve):
            def norm_moments(v, stats, stats_done, moments, moments_done, group):
                for b in range(B):
                    last = nc.vector.bn_stats(stats[:, b, :], v[:, b, :])
                last.then_inc(stats_done, 1)
                dve.drain()
                for b in range(B):
                    last = nc.vector.bn_aggr(moments[:, b, :], stats[:, b, :])
                last.then_inc(moments_done, 1)

            def normalise(v, moments, rstd, rstd_done, xhat, xhat_done, group):
                dve.wait_ge(rstd_done, group + 1)
                for b in range(B):
                    last = nc.vector.tensor_scalar(xhat[:, b, :], v[:, b, :], moments[:, b, 0:1], rstd[:, b:b + 1],
                                                   ALU.subtract, ALU.mult)
                last.then_inc(xhat_done, 1)

            def first_norm(group, parity, overwrites):
                dve.wait_ge(x_loaded[parity], landed(group, parity))
                norm_moments(x_sb[parity], stats1, stats1_done, moments1, moments1_done, group)
                if overwrites:
                    dve.wait_ge(ax_product, group)
                normalise(x_sb[parity], moments1, rstd1, rstd1_done, xhat1, xhat1_done, group)

            def gate_expert(m, parity, e):
                dve.wait_ge(hid_ready, m * E + e + 1)
                if e == 0:
                    dve.wait_ge(gate_loaded[parity], landed(m, parity))
                if e >= GATED_BUFS:
                    dve.wait_ge(down_done, m * E + e - GATED_BUFS + 1)
                nc.vector.tensor_tensor(gated[e % GATED_BUFS][:], hid[e % HID_BUFS][:], gate[parity][:, e, :],
                                        ALU.mult).then_inc(gated_ready, 1)

            def shift_logits(c):
                links = [0]

                def link(instruction):
                    links[0] += 1
                    instruction.then_inc(softmax_link, 1)
                    dve.wait_ge(softmax_link, c * SOFTMAX_LINKS + links[0])

                dve.wait_ge(logits_product, c + 1)
                parts = route_ps[:, 0:B * 2 * E].rearrange("p (b k e) -> p b e k", b=B, k=2)
                link(nc.vector.tensor_reduce(logits[:], parts, AX, ALU.add))
                link(nc.vector.tensor_reduce(top_logit[:], logits[:], AX, ALU.max))
                nc.vector.tensor_tensor(shifted[:], logits[:], top_logit[:].unsqueeze(2).to_broadcast([P, B, E]),
                                        ALU.subtract).then_inc(shifted_done, 1)
                return links[0]

            def select_experts(c, links_before):
                links = [links_before]

                def link(instruction, alone=False):
                    links[0] += 1
                    instruction.then_inc(softmax_link, 1)
                    if alone:
                        dve.drain()
                        return
                    dve.wait_ge(softmax_link, c * SOFTMAX_LINKS + links[0])

                dve.wait_ge(exps_done, c + 1)
                link(nc.vector.tensor_reduce(exp_sum[:], exps[:], AX, ALU.add))
                link(nc.vector.reciprocal(exp_inv[:], exp_sum[:]))
                link(nc.vector.tensor_tensor(probs[:], exps[:], exp_inv[:].unsqueeze(2).to_broadcast([P, B, E]),
                                             ALU.mult), alone=True)
                for b in range(B):
                    last = nc.vector.max(best[:, b, :], probs[:, b, :])
                link(last, alone=True)
                for b in range(B):
                    last = nc.vector.max_index(best_at[:, b, :], best[:, b, :], probs[:, b, :])
                link(last)
                nc.vector.tensor_copy(best_id[:], best_at[:, :, 0:TOP])
                link(nc.vector.tensor_tensor(pair_sum[:], best[:, :, 0], best[:, :, 1], ALU.add))
                link(nc.vector.tensor_scalar(pair_inv[:], pair_sum[:], GUARD, None, ALU.max))
                link(nc.vector.reciprocal(pair_sum[:], pair_inv[:]))
                nc.vector.tensor_tensor(pair_w[:], best[:, :, 0:TOP], pair_sum[:].unsqueeze(2).to_broadcast([P, B, TOP]),
                                        ALU.mult)
                link(nc.vector.tensor_tensor(
                    chosen[:], expert_id[:].unsqueeze(1).unsqueeze(1).to_broadcast([P, B, TOP, E]),
                    best_id[:].unsqueeze(3).to_broadcast([P, B, TOP, E]), ALU.is_equal))
                link(nc.vector.tensor_tensor(weighed[:], chosen[:], pair_w[:].unsqueeze(3).to_broadcast([P, B, TOP, E]),
                                             ALU.mult))
                assert links[0] == SOFTMAX_LINKS
                if not (isinstance(c, int) and c == 0):
                    dve.wait_ge(ct_product, c)
                nc.vector.tensor_tensor(combine[:], weighed[:, :, 0, :], weighed[:, :, 1, :], ALU.add).then_inc(combine_done, 1)

            def step(s, parity, graph, norm_next, select, experts):
                c, m = s - 1, s - 2
                if select:
                    links = shift_logits(c)
                if experts:
                    gate_expert(m, parity, 0)
                    gate_expert(m, parity, 1)
                if graph:
                    for k in range(C1):
                        dve.wait_ge(ah_hi_ready, s * C1 + k + 1)
                        nc.vector.tensor_tensor(ah_lo[:, k, :], pair_ps[k][:], ah_hi[:, k, :].bitcast(f32),
                                                ALU.subtract).then_inc(ah_lo_ready, 1)
                if experts:
                    gate_expert(m, parity, 2)
                if select:
                    select_experts(c, links)
                if norm_next:
                    first_norm(s + 1, 1 - parity, True)
                if experts:
                    gate_expert(m, parity, 3)
                if graph:
                    dve.wait_ge(as3_product, s + 1)
                    if not (isinstance(s, int) and s == 0):
                        dve.wait_ge(base_done, s)
                    nc.vector.tensor_tensor(x1[:].rearrange("p b f -> p (b f)"), chain_ps[:],
                                            x_sb[parity][:].rearrange("p b f -> p (b f)"), ALU.add).then_inc(x1_done, 1)
                if experts:
                    gate_expert(m, parity, 4)
                if graph:
                    dve.wait_ge(x1_done, s + 1)
                    norm_moments(x1, stats2, stats2_done, moments2, moments2_done, s)
                if experts:
                    gate_expert(m, parity, 5)
                    gate_expert(m, parity, 6)
                if graph:
                    normalise(x1, moments2, rstd2, rstd2_done, xhat2, xhat2_done, s)
                if experts:
                    gate_expert(m, parity, 7)
                if graph:
                    dve.wait_ge(xt_hi_ready, s + 1)
                    nc.vector.tensor_tensor(xt_lo[parity][:], chain_ps[:], xt_hi[parity][:].bitcast(f32),
                                            ALU.subtract).then_inc(xt_lo_ready, 1)
                if experts:
                    dve.wait_ge(y_product, m + 1)
                    dve.wait_ge(base_done, m + 1)
                    if not (isinstance(m, int) and m < 2):
                        dve.wait_ge(out_stored[parity], (m - parity) * (DONE // 2))
                    nc.vector.tensor_tensor(out_sb[parity][:].rearrange("p b f -> p (b f)"), y_ps[:],
                                            base[parity][:].rearrange("p b f -> p (b f)"), ALU.add).then_inc(out_ready, 1)

            dve.wait_ge(graph_loaded, DONE)
            nc.vector.tensor_tensor(a_t[:], adj_sb[:], adj_sb[:], ALU.mult).then_inc(a_ready, 1)
            first_norm(0, 0, False)
            dve.wait_ge(w2_loaded, DONE)
            nc.vector.tensor_copy(w2_hi[:], w2_raw[:]).then_inc(w2_split_hi, 1)
            dve.wait_ge(w2_split_hi, 1)
            nc.vector.tensor_tensor(w2_lo[:], w2_raw[:], w2_hi[:].bitcast(f32), ALU.subtract).then_inc(w2_split, 1)
            dve.wait_ge(ffn_loaded, 5 * DONE)
            nc.vector.tensor_copy(router[:, 0, :], router_raw[:])
            nc.vector.tensor_copy(up_hi[:], up_raw[:]).then_inc(ffn_split_hi, 1)
            dve.wait_ge(ffn_split_hi, 1)
            nc.vector.tensor_tensor(router[:, 1, :], router_raw[:], router[:, 0, :].bitcast(f32), ALU.subtract)
            nc.vector.tensor_tensor(up_lo[:], up_raw[:], up_hi[:].bitcast(f32), ALU.subtract).then_inc(ffn_split, 1)
            dve.wait_ge(consts_ready, 1)
            run_steps(dve, step)

        @block.scalar
        def _(act):
            def expert_hidden(m, e):
                act.wait_ge(hid_product, m * E + e + 1)
                if e >= HID_BUFS:
                    act.wait_ge(gated_ready, m * E + e - HID_BUFS + 1)
                nc.scalar.activation(hid[e % HID_BUFS][:], hid_ps[e % 2][:], ACT.Gelu,
                                     bias=b1_sb[:, e:e + 1]).then_inc(hid_ready, 1)

            def step(s, parity, graph, norm_next, select, experts):
                c, m = s - 1, s - 2
                if graph:
                    act.wait_ge(ax_product, s + 1)
                    nc.scalar.activation(ax_t[:], chain_ps[:], ACT.Copy).then_inc(ax_ready, 1)
                if experts:
                    expert_hidden(m, 0)
                if graph:
                    for k in range(2):
                        act.wait_ge(h1_product, s * 2 + k + 1)
                        nc.scalar.activation(h1[:, 2 * k:2 * k + 2, :].rearrange("p b h -> p (b h)"), pair_ps[k][:],
                                             ACT.Relu).then_inc(h1_ready, 1)
                if experts:
                    expert_hidden(m, 1)
                if graph:
                    for k in range(C1):
                        act.wait_ge(ah_product, s * C1 + k + 1)
                        nc.scalar.activation(ah_hi[:, k, :], pair_ps[k][:], ACT.Copy).then_inc(ah_hi_ready, 1)
                if experts:
                    expert_hidden(m, 2)
                if graph:
                    for j in range(C2):
                        act.wait_ge(h2_product, s * C2 + j + 1)
                        nc.scalar.activation(h2_t[:, j, :], pair_ps[j % 2][:], ACT.Relu).then_inc(h2_ready, 1)
                if experts:
                    expert_hidden(m, 3)
                if graph:
                    act.wait_ge(s3_product, s + 1)
                    nc.scalar.activation(s3[:].rearrange("p b f -> p (b f)"), chain_ps[:], ACT.Copy).then_inc(s3_ready, 1)

                def combine_out():
                    act.wait_ge(ct_product, c + 1)
                    if not (isinstance(c, int) and c == 0):
                        act.wait_ge(ct_stored, c * DONE)
                    nc.scalar.activation(ct_sb[:], route_ps[0:E, :], ACT.Copy).then_inc(ct_ready, 1)

                if select and graph:
                    combine_out()
                if experts:
                    for e in range(4, E):
                        expert_hidden(m, e)
                if select and not graph:
                    combine_out()
                if experts:
                    act.wait_ge(down_done, (m + 1) * E)
                    nc.scalar.activation(yt_sb[:], yt_ps[:], ACT.Copy).then_inc(yt_ready, 1)
                if graph:
                    act.wait_ge(xt_product, s + 1)
                    nc.scalar.activation(xt_hi[parity][:], chain_ps[:], ACT.Copy).then_inc(xt_hi_ready, 1)

            act.wait_ge(ffn_loaded, 5 * DONE)
            run_steps(act, step)

        @block.tensor
        def _(pe):
            def three_passes(dst, w_hi, w_lo, v_hi, v_lo, start, stop):
                nc.tensor.matmul(dst, w_hi, v_hi, start=start, stop=False)
                nc.tensor.matmul(dst, w_hi, v_lo, start=False, stop=False)
                return nc.tensor.matmul(dst, w_lo, v_hi, start=False, stop=stop)

            def expert_up(m, parity, e):
                if e >= 2:
                    pe.wait_ge(hid_ready, m * E + e - 1)
                three_passes(hid_ps[e % 2][:], up_hi[:, e, :], up_lo[:, e, :], xt_hi[parity][:], xt_lo[parity][:],
                             True, True).then_inc(hid_product, 1)

            def expert_down(m, e):
                pe.wait_ge(gated_ready, m * E + e + 1)
                nc.tensor.matmul(yt_ps[:], down[:, e, :], gated[e % GATED_BUFS][:], start=False,
                                 stop=(e == E - 1)).then_inc(down_done, 1)

            def graph_hidden2(s, j):
                if j == 0:
                    pe.wait_ge(ah_lo_ready, (s + 1) * C1)
                if j >= 2:
                    pe.wait_ge(h2_ready, s * C2 + j - 1)
                for k in range(C1):
                    last = three_passes(pair_ps[j % 2][:], w2_hi[:, k, j * P:(j + 1) * P], w2_lo[:, k, j * P:(j + 1) * P],
                                        ah_hi[:, k, :], ah_lo[:, k, :], k == 0, k == C1 - 1)
                last.then_inc(h2_product, 1)

            def graph_out(s, j):
                pe.wait_ge(h2_ready, s * C2 + j + 1)
                for b in range(B):
                    last = nc.tensor.matmul(chain_ps[:, b * F:(b + 1) * F], h2_t[:, j, b * P:(b + 1) * P], w3g[:, j, :],
                                            start=(j == 0 and b == 0), stop=(j == C2 - 1), skip_group_check=True)
                return last

            def step(s, parity, graph, norm_next, select, experts):
                c, m = s - 1, s - 2
                if graph:
                    pe.wait_ge(xhat1_done, s + 1)
                    for b in range(B):
                        last = nc.tensor.matmul(chain_ps[:, b * P:(b + 1) * P], xhat1[:, b, :], a_t[:], start=True, stop=True)
                    last.then_inc(ax_product, 1)
                if experts:
                    nc.tensor.matmul(yt_ps[:], b2_sb[:], ct_sb[:], start=True, stop=False)
                    expert_up(m, parity, 0)
                if graph:
                    pe.wait_ge(ax_ready, s + 1)
                    for b in range(B):
                        at = (b % 2) * H1
                        last = nc.tensor.matmul(pair_ps[b // 2][:, at:at + H1], ax_t[:, b * P:(b + 1) * P], w1g[:],
                                                start=True, stop=True)
                        if b % 2:
                            last.then_inc(h1_product, 1)
                if experts:
                    expert_up(m, parity, 1)
                    expert_down(m, 0)
                if graph:
                    pe.wait_ge(h1_ready, (s + 1) * 2)
                    for k in range(C1):
                        for b in range(B):
                            last = nc.tensor.matmul(pair_ps[k][:, b * P:(b + 1) * P], h1[:, b, k * P:(k + 1) * P], a_t[:],
                                                    start=True, stop=True)
                        last.then_inc(ah_product, 1)
                if experts:
                    expert_up(m, parity, 2)
                    expert_down(m, 1)
                if graph:
                    graph_hidden2(s, 0)
                    for j in range(1, C2):
                        graph_hidden2(s, j)
                        graph_out(s, j - 1)
                if experts:
                    expert_up(m, parity, 3)
                if graph:
                    graph_out(s, C2 - 1).then_inc(s3_product, 1)

                def combine_across():
                    pe.wait_ge(combine_done, c + 1)
                    for b in range(B):
                        last = nc.tensor.transpose(route_ps[0:E, b * P:(b + 1) * P], combine[:, b, :], ident[:])
                    last.then_inc(ct_product, 1)

                if select and graph:
                    combine_across()
                if experts:
                    expert_down(m, 2)
                    expert_up(m, parity, 4)
                if graph:
                    pe.wait_ge(s3_ready, s + 1)
                    nc.tensor.matmul(chain_ps[:], a_t[:], s3[:].rearrange("p b f -> p (b f)"), start=True,
                                     stop=True).then_inc(as3_product, 1)
                if experts:
                    for e in range(5, E):
                        expert_down(m, e - 2)
                        expert_up(m, parity, e)
                    expert_down(m, E - 2)
                    expert_down(m, E - 1)
                if select and not graph:
                    combine_across()
                if graph:
                    pe.wait_ge(xhat2_done, s + 1)
                    for b in range(B):
                        last = nc.tensor.transpose(chain_ps[:, b * P:(b + 1) * P], xhat2[:, b, :], ident[:])
                    last.then_inc(xt_product, 1)
                if experts:
                    pe.wait_ge(yt_ready, m + 1)
                    for b in range(B):
                        last = nc.tensor.transpose(y_ps[:, b * F:(b + 1) * F], yt_sb[:, b * P:(b + 1) * P], ident[:])
                    last.then_inc(y_product, 1)
                if graph:
                    pe.wait_ge(xt_lo_ready, s + 1)
                    if select:
                        pe.wait_ge(ct_ready, s)
                    weights = router[:].rearrange("p k e -> p (k e)")
                    for b in range(B):
                        dst = route_ps[:, b * 2 * E:(b + 1) * 2 * E]
                        nc.tensor.matmul(dst, xt_hi[parity][:, b * P:(b + 1) * P], weights, start=True, stop=False)
                        last = nc.tensor.matmul(dst, xt_lo[parity][:, b * P:(b + 1) * P], weights, start=False, stop=True)
                    last.then_inc(logits_product, 1)

            pe.wait_ge(a_ready, 1)
            pe.wait_ge(w1_loaded, DONE)
            pe.wait_ge(w3_loaded, DONE)
            pe.wait_ge(consts_ready, 1)
            pe.wait_ge(w2_split, 1)
            pe.wait_ge(ffn_split, 1)
            run_steps(pe, step)


_OUT = "out_dram"


def kernel(x, adj, L0_gnn_W1, L0_gnn_W2, L0_gnn_W3, L0_ffn_router_w, L0_ffn_w1, L0_ffn_b1, L0_ffn_w2, L0_ffn_b2):
    import numpy as np
    import concourse.bacc as bacc
    from concourse import mybir as mb
    from concourse.bass_utils import run_bass_kernel_spmd

    batches, nodes, features = x.shape
    per_group = 4
    groups = batches // per_group

    def grouped(a):
        return a.reshape(groups, per_group, nodes, features).transpose(0, 2, 1, 3).reshape(groups, nodes, -1)

    laid_out = {
        "x": grouped(np.asarray(x)),
        "adj_t": np.asarray(adj).T,
        "gnn_w1": np.asarray(L0_gnn_W1),
        "gnn_w2": np.asarray(L0_gnn_W2),
        "gnn_w3": np.asarray(L0_gnn_W3),
        "router_t": np.asarray(L0_ffn_router_w).T,
        "ffn_w1": np.asarray(L0_ffn_w1).transpose(1, 0, 2),
        "ffn_b1_t": np.asarray(L0_ffn_b1).T,
        "ffn_w2": np.asarray(L0_ffn_w2).transpose(1, 0, 2),
        "ffn_b2": np.asarray(L0_ffn_b2),
    }
    nc = bacc.Bacc("TRN2", target_bir_lowering=False, num_devices=1)
    arrays, args = {}, []
    for name, a in laid_out.items():
        a = np.ascontiguousarray(a)
        arrays[f"in_{name}"] = a
        args.append(nc.dram_tensor(f"in_{name}", a.shape, mb.dt.from_np(a.dtype), kind="ExternalInput").ap())
    out = nc.dram_tensor(_OUT, (groups, nodes, per_group * features), mb.dt.float32, kind="ExternalOutput").ap()
    gnn_moe_kernel(nc, *args, out)
    result = run_bass_kernel_spmd(nc, [arrays], core_ids=[0]).results[0][_OUT]
    return (result.reshape(groups, nodes, per_group, features).transpose(0, 2, 1, 3)
            .reshape(batches, nodes, features))
```

```python
import concourse.bass as bass
from concourse import mybir
from concourse.alu_op_type import AluOpType as ALU
from contextlib import ExitStack


def gnn_moe_kernel(
    nc: bass.Bass,
    x: bass.AP,
    adj_t: bass.AP,
    gnn_w1: bass.AP,
    gnn_w2: bass.AP,
    gnn_w3: bass.AP,
    router_t: bass.AP,
    ffn_w1: bass.AP,
    ffn_b1_t: bass.AP,
    ffn_w2: bass.AP,
    ffn_b2: bass.AP,
    out: bass.AP,
):
    f32 = mybir.dt.float32
    f32r = mybir.dt.float32r
    u32 = mybir.dt.uint32
    ACT = mybir.ActivationFunctionType
    AX = mybir.AxisListType.X

    GROUPS, P, GF = x.shape
    F = gnn_w1.shape[0]
    B = GF // F
    T = B * P
    H1 = gnn_w1.shape[1]
    H2 = gnn_w2.shape[1]
    C1 = H1 // P
    C2 = H2 // P
    E = ffn_w1.shape[1]
    TOP = 2
    BANK = 512
    BN = 6
    EPS = 1e-5
    GUARD = 1e-12
    DONE = 16
    HID_BUFS = 2
    GATED_BUFS = 4
    PARTS = 4
    LOOP_FROM, LOOP_TO = 4, GROUPS - 2

    ctx = ExitStack()
    with ctx:
        def sb(name, shape, dt=f32):
            return ctx.enter_context(nc.sbuf_tensor(name, shape, dt))

        def pb(name):
            return ctx.enter_context(nc.psum_tensor(name, [P, BANK], f32))

        def sem(name):
            return ctx.enter_context(nc.semaphore(name))

        ident = sb("ident", [P, P])
        expert_id = sb("expert_id", [P, E])
        neg_half = sb("neg_half", [P, B])
        eps = sb("eps", [P, B])
        euler = sb("euler", [P, B * E])
        adj_sb = sb("adj_sb", [P, P])
        a_t = sb("a_t", [P, P])
        w1_raw = sb("w1_raw", [P, H1])
        w1_hi = sb("w1_hi", [P, H1], f32r)
        w1_lo = sb("w1_lo", [P, H1], f32r)
        w2_raw = sb("w2_raw", [P, C1, H2])
        w2_hi = sb("w2_hi", [P, C1, H2], f32r)
        w2_lo = sb("w2_lo", [P, C1, H2], f32r)
        w3g = sb("w3g", [P, C2, F])
        up_raw = sb("up_raw", [P, E, P])
        up_hi = sb("up_hi", [P, E, P], f32r)
        up_lo = sb("up_lo", [P, E, P], f32r)
        down_raw = sb("down_raw", [P, E, F])
        down_hi = sb("down_hi", [P, E, F], f32r)
        down_lo = sb("down_lo", [P, E, F], f32r)
        b1_sb = sb("b1_sb", [P, E])
        b2_raw = sb("b2_raw", [PARTS * E, F])
        b2_lo = sb("b2_lo", [PARTS * E, F], f32r)
        b2_parts = sb("b2_parts", [PARTS * E, F], f32r)
        router_raw = sb("router_raw", [P, E])
        router = sb("router", [P, 2, E], f32r)

        x_sb = [sb(f"x_sb{i}", [P, B, F]) for i in range(2)]
        xhat1 = sb("xhat1", [P, B, F])
        stats1 = sb("stats1", [P, B, BN])
        moments1 = sb("moments1", [P, B, 2])
        var1 = sb("var1", [P, B])
        rstd1 = sb("rstd1", [P, B])
        ax_hi = sb("ax_hi", [P, T], f32r)
        ax_lo = sb("ax_lo", [P, T], f32r)
        h1 = sb("h1", [P, B, H1])
        ah_hi = sb("ah_hi", [P, C1, T], f32r)
        ah_lo = sb("ah_lo", [P, C1, T], f32r)
        h2_t = sb("h2_t", [P, C2, T])
        s3 = sb("s3", [P, B, F])
        x1 = sb("x1", [P, B, F])
        xhat2 = sb("xhat2", [P, B, F])
        stats2 = sb("stats2", [P, B, BN])
        moments2 = sb("moments2", [P, B, 2])
        var2 = sb("var2", [P, B])
        rstd2 = sb("rstd2", [P, B])
        base = [sb(f"base{i}", [P, B, F]) for i in range(2)]
        xt_hi = [sb(f"xt_hi{i}", [P, T], f32r) for i in range(2)]
        xt_lo = [sb(f"xt_lo{i}", [P, T], f32r) for i in range(2)]
        logits = sb("logits", [P, B, E])
        top_logit = sb("top_logit", [P, B])
        shifted = sb("shifted", [P, B, E])
        exps = sb("exps", [P, B, E])
        exp_sum = sb("exp_sum", [P, B])
        exp_inv = sb("exp_inv", [P, B])
        probs = sb("probs", [P, B, E])
        best = sb("best", [P, B, 8])
        best_at = sb("best_at", [P, B, 8], u32)
        best_id = sb("best_id", [P, B, TOP])
        pair_sum = sb("pair_sum", [P, B])
        pair_inv = sb("pair_inv", [P, B])
        pair_w = sb("pair_w", [P, B, TOP])
        chosen = sb("chosen", [P, B, TOP, E])
        weighed = sb("weighed", [P, B, TOP, E])
        combine = sb("combine", [P, B, PARTS, E])
        ct_sb = sb("ct_sb", [E, T])
        ct_parts = sb("ct_parts", [PARTS * E, T], f32r)
        gate = [sb(f"gate{i}", [P, E, T]) for i in range(2)]
        hid = [sb(f"hid{i}", [P, T]) for i in range(HID_BUFS)]
        gated = [sb(f"gated{i}", [P, T]) for i in range(GATED_BUFS)]
        gated_hi = [sb(f"gated_hi{i}", [P, T], f32r) for i in range(E)]
        gated_lo = [sb(f"gated_lo{i}", [P, T], f32r) for i in range(E)]
        yt_sb = sb("yt_sb", [P, T])
        out_sb = [sb(f"out_sb{i}", [P, B, F]) for i in range(2)]
        ct_dram = nc.dram_tensor("ct_dram", [GROUPS, E, T], f32, kind="Internal").ap()

        chain_ps = pb("chain_ps")
        pair_ps = [pb(f"pair_ps{i}") for i in range(2)]
        turn_ps = pb("turn_ps")
        route_ps = pb("route_ps")
        hid_ps = [pb(f"hid_ps{i}") for i in range(2)]
        yt_ps = pb("yt_ps")

        graph_loaded = sem("graph_loaded")
        w1_loaded = sem("w1_loaded")
        w2_loaded = sem("w2_loaded")
        w3_loaded = sem("w3_loaded")
        router_loaded = sem("router_loaded")
        b1_loaded = sem("b1_loaded")
        b2_loaded = sem("b2_loaded")
        up_loaded = sem("up_loaded")
        down_loaded = sem("down_loaded")
        x_loaded = [sem(f"x_loaded{i}") for i in range(2)]
        ct_stored = sem("ct_stored")
        gate_loaded = [sem(f"gate_loaded{i}") for i in range(2)]
        out_stored = [sem(f"out_stored{i}") for i in range(2)]
        ident_zero = sem("ident_zero")
        consts_ready = sem("consts_ready")
        ids_int = sem("ids_int")
        a_ready = sem("a_ready")
        w1_split_hi = sem("w1_split_hi")
        w1_split = sem("w1_split")
        w2_split_hi = sem("w2_split_hi")
        w2_split = sem("w2_split")
        router_split_hi = sem("router_split_hi")
        router_split = sem("router_split")
        b2_zero = sem("b2_zero")
        b2_split_hi = sem("b2_split_hi")
        b2_split = sem("b2_split")
        b2_stacked = sem("b2_stacked")
        ffn_split_hi = sem("ffn_split_hi")
        ffn_split = sem("ffn_split")
        moments1_done = sem("moments1_done")
        var1_done = sem("var1_done")
        rstd1_done = sem("rstd1_done")
        xhat1_done = sem("xhat1_done")
        ax_product = sem("ax_product")
        ax_hi_ready = sem("ax_hi_ready")
        ax_lo_ready = sem("ax_lo_ready")
        h1_product = sem("h1_product")
        h1_ready = sem("h1_ready")
        ah_product = sem("ah_product")
        ah_hi_ready = sem("ah_hi_ready")
        ah_lo_ready = sem("ah_lo_ready")
        h2_product = sem("h2_product")
        h2_ready = sem("h2_ready")
        s3_product = sem("s3_product")
        s3_ready = sem("s3_ready")
        as3_product = sem("as3_product")
        x1_done = sem("x1_done")
        moments2_done = sem("moments2_done")
        var2_done = sem("var2_done")
        rstd2_done = sem("rstd2_done")
        xhat2_done = sem("xhat2_done")
        base_done = sem("base_done")
        xt_product = sem("xt_product")
        xt_hi_ready = sem("xt_hi_ready")
        xt_lo_ready = sem("xt_lo_ready")
        logits_product = sem("logits_product")
        softmax_link = sem("softmax_link")
        shifted_done = sem("shifted_done")
        exps_done = sem("exps_done")
        combine_done = sem("combine_done")
        ct_product = sem("ct_product")
        ct_ready = sem("ct_ready")
        hid_product = sem("hid_product")
        hid_ready = sem("hid_ready")
        gated_ready = sem("gated_ready")
        gated_hi_ready = sem("gated_hi_ready")
        gated_lo_ready = sem("gated_lo_ready")
        down_done = sem("down_done")
        yt_ready = sem("yt_ready")
        y_product = sem("y_product")
        out_ready = sem("out_ready")

        SOFTMAX_LINKS = 14

        def run_steps(eng, step):
            step(0, 0, graph=True, next_group=True, select=False, experts=False)
            step(1, 1, graph=True, next_group=True, select=True, experts=False)
            step(2, 0, graph=True, next_group=True, select=True, experts=True)
            step(3, 1, graph=True, next_group=True, select=True, experts=True)
            with eng.Fori(LOOP_FROM, LOOP_TO, 2) as s:
                for parity in range(2):
                    step(s + parity, parity, graph=True, next_group=True, select=True, experts=True)
            step(LOOP_TO, 0, graph=True, next_group=True, select=True, experts=True)
            step(LOOP_TO + 1, 1, graph=True, next_group=False, select=True, experts=True)
            step(GROUPS, 0, graph=False, next_group=False, select=True, experts=True)
            step(GROUPS + 1, 1, graph=False, next_group=False, select=False, experts=True)

        def landed(group, parity, dmas=1):
            return (group - parity) * (DONE * dmas // 2) + DONE * dmas

        block = ctx.enter_context(nc.Block())

        @block.sync
        def _(sp):
            sp.dma_start(x_sb[0][:], x[0].rearrange("p (b f) -> p b f", b=B)).then_inc(x_loaded[0], DONE)
            sp.dma_start(adj_sb[:], adj_t).then_inc(graph_loaded, DONE)
            sp.dma_start(w1_raw[:], gnn_w1).then_inc(w1_loaded, DONE)
            sp.dma_start(w2_raw[:], gnn_w2.rearrange("(c p) h -> p c h", p=P)).then_inc(w2_loaded, DONE)
            sp.dma_start(w3g[:], gnn_w3.rearrange("(c p) f -> p c f", p=P)).then_inc(w3_loaded, DONE)
            sp.dma_start(router_raw[:], router_t).then_inc(router_loaded, DONE)
            sp.dma_start(b1_sb[:], ffn_b1_t).then_inc(b1_loaded, DONE)
            sp.wait_ge(b2_zero, 1)
            for part in range(1, PARTS):
                sp.dma_start(b2_raw[part * E:(part + 1) * E, :], ffn_b2).then_inc(b2_loaded, DONE)
            sp.dma_start(up_raw[:], ffn_w1).then_inc(up_loaded, DONE)
            sp.dma_start(down_raw[:], ffn_w2).then_inc(down_loaded, DONE)
            sp.wait_ge(b2_split, 1)
            last_rows = slice((PARTS - 1) * E, PARTS * E)
            sp.dma_start(b2_parts[last_rows, :].bitcast(f32), b2_lo[last_rows, :].bitcast(f32)).then_inc(b2_stacked, DONE)

            def step(s, parity, graph, next_group, select, experts):
                c, m = s - 1, s - 2
                if next_group:
                    x_from = x[bass.ds(s + 1, 1)].rearrange("o p (b f) -> (o p) b f", b=B)
                    if not (isinstance(s, int) and s == 0):
                        sp.wait_ge(x1_done, s)
                    sp.dma_start(x_sb[1 - parity][:], x_from).then_inc(x_loaded[1 - parity], DONE)
                if select:
                    ct_to = ct_dram[bass.ds(c, 1)].rearrange("o e t -> (o e) t")
                    gate_from = (ct_dram[bass.ds(c, 1)].rearrange("o e t -> o (e t)").partition_broadcast(P)
                                 .rearrange("p o (e t) -> p (o e) t", e=E))
                    if not (isinstance(s, int) and s < 3):
                        sp.wait_ge(yt_ready, c - 1)
                    sp.wait_ge(ct_ready, c + 1)
                    sp.dma_start(ct_to, ct_sb[:]).then_inc(ct_stored, DONE)
                    sp.wait_ge(ct_stored, (c + 1) * DONE)
                    sp.dma_start(gate[1 - parity][:], gate_from).then_inc(gate_loaded[1 - parity], DONE)
                if experts:
                    out_to = out[bass.ds(m, 1)].rearrange("o p (b f) -> (o p) b f", b=B)
                    sp.wait_ge(out_ready, m + 1)
                    sp.dma_start(out_to, out_sb[parity][:]).then_inc(out_stored[parity], DONE)

            run_steps(sp, step)
            for parity in range(2):
                sp.wait_ge(out_stored[parity], GROUPS // 2 * DONE)

        @block.gpsimd
        def _(pool):
            nc.gpsimd.memset(b2_raw[:], 0.0).then_inc(b2_zero, 1)
            nc.gpsimd.memset(ident[:], 0.0).then_inc(ident_zero, 1)
            nc.gpsimd.memset(neg_half[:], -0.5)
            nc.gpsimd.memset(eps[:], EPS)
            nc.gpsimd.memset(euler[:], 2.718281828459045)
            nc.gpsimd.iota(best_at[:, 0, 0:E], pattern=[[1, E]], base=0, channel_multiplier=0).then_inc(ids_int, 1)
            pool.wait_ge(ids_int, 1)
            nc.gpsimd.tensor_copy(expert_id[:], best_at[:, 0, 0:E])
            pool.wait_ge(ident_zero, 1)
            nc.gpsimd.affine_select(out=ident[:], in_=ident[:], compare_op=ALU.not_equal, fill=1.0, base=0,
                                    pattern=[[-1, P]], channel_multiplier=1).then_inc(consts_ready, 1)

            def root(group, moments_done, moments, var, var_done, rstd, rstd_done):
                pool.wait_ge(moments_done, group + 1)
                nc.gpsimd.tensor_tensor(var[:], moments[:, :, 1], eps[:], ALU.add).then_inc(var_done, 1)
                pool.wait_ge(var_done, group + 1)
                nc.gpsimd.tensor_tensor(rstd[:], var[:], neg_half[:], ALU.pow).then_inc(rstd_done, 1)

            def step(s, parity, graph, next_group, select, experts):
                if select:
                    pool.wait_ge(shifted_done, s)
                    nc.gpsimd.tensor_tensor(exps[:].rearrange("p b e -> p (b e)"), euler[:],
                                            shifted[:].rearrange("p b e -> p (b e)"), ALU.pow).then_inc(exps_done, 1)
                if next_group:
                    root(s + 1, moments1_done, moments1, var1, var1_done, rstd1, rstd1_done)
                if graph:
                    root(s, moments2_done, moments2, var2, var2_done, rstd2, rstd2_done)
                    pool.wait_ge(xhat2_done, s + 1)
                    if experts:
                        pool.wait_ge(out_ready, s - 1)
                    nc.gpsimd.tensor_tensor(base[parity][:], x1[:], xhat2[:], ALU.add).then_inc(base_done, 1)

            pool.wait_ge(consts_ready, 1)
            root(0, moments1_done, moments1, var1, var1_done, rstd1, rstd1_done)
            run_steps(pool, step)

        @block.vector
        def _(dve):
            def norm_moments(v, stats, moments, moments_done):
                for b in range(B):
                    nc.vector.bn_stats(stats[:, b, :], v[:, b, :])
                dve.drain()
                for b in range(B):
                    last = nc.vector.bn_aggr(moments[:, b, :], stats[:, b, :])
                last.then_inc(moments_done, 1)

            def normalise(v, moments, rstd, rstd_done, xhat, xhat_done, group):
                dve.wait_ge(rstd_done, group + 1)
                for b in range(B):
                    last = nc.vector.tensor_scalar(xhat[:, b, :], v[:, b, :], moments[:, b, 0:1], rstd[:, b:b + 1],
                                                   ALU.subtract, ALU.mult)
                last.then_inc(xhat_done, 1)

            def first_moments(group, parity):
                dve.wait_ge(x_loaded[parity], landed(group, parity))
                norm_moments(x_sb[parity], stats1, moments1, moments1_done)

            def first_norm(group, parity):
                if not (isinstance(group, int) and group == 0):
                    dve.wait_ge(ax_product, group)
                normalise(x_sb[parity], moments1, rstd1, rstd1_done, xhat1, xhat1_done, group)

            def round_off(lo, value, hi, hi_ready, count, lo_ready):
                dve.wait_ge(hi_ready, count)
                nc.vector.tensor_tensor(lo, value, hi.bitcast(f32), ALU.subtract).then_inc(lo_ready, 1)

            def gate_expert(m, parity, e):
                dve.wait_ge(hid_ready, m * E + e + 1)
                if e == 0:
                    dve.wait_ge(gate_loaded[parity], landed(m, parity))
                nc.vector.tensor_tensor(gated[e % GATED_BUFS][:], hid[e % HID_BUFS][:], gate[parity][:, e, :],
                                        ALU.mult).then_inc(gated_ready, 1)

            def gate_low(m, e):
                round_off(gated_lo[e][:], gated[e % GATED_BUFS][:], gated_hi[e][:], gated_hi_ready, m * E + e + 1,
                          gated_lo_ready)

            def shift_logits(c):
                links = [0]

                def link(instruction):
                    links[0] += 1
                    instruction.then_inc(softmax_link, 1)
                    dve.wait_ge(softmax_link, c * SOFTMAX_LINKS + links[0])

                dve.wait_ge(logits_product, c + 1)
                parts = route_ps[:, 0:B * 2 * E].rearrange("p (b k e) -> p b e k", b=B, k=2)
                link(nc.vector.tensor_reduce(logits[:], parts, AX, ALU.add))
                link(nc.vector.tensor_reduce(top_logit[:], logits[:], AX, ALU.max))
                nc.vector.tensor_tensor(shifted[:], logits[:], top_logit[:].unsqueeze(2).to_broadcast([P, B, E]),
                                        ALU.subtract).then_inc(shifted_done, 1)
                return links[0]

            def select_experts(c, links_before):
                links = [links_before]

                def link(instruction, alone=False):
                    links[0] += 1
                    instruction.then_inc(softmax_link, 1)
                    if alone:
                        dve.drain()
                        return
                    dve.wait_ge(softmax_link, c * SOFTMAX_LINKS + links[0])

                dve.wait_ge(exps_done, c + 1)
                link(nc.vector.tensor_reduce(exp_sum[:], exps[:], AX, ALU.add))
                link(nc.vector.reciprocal(exp_inv[:], exp_sum[:]))
                link(nc.vector.tensor_tensor(probs[:], exps[:], exp_inv[:].unsqueeze(2).to_broadcast([P, B, E]),
                                             ALU.mult), alone=True)
                for b in range(B):
                    last = nc.vector.max(best[:, b, :], probs[:, b, :])
                link(last, alone=True)
                for b in range(B):
                    last = nc.vector.max_index(best_at[:, b, :], best[:, b, :], probs[:, b, :])
                link(last)
                nc.vector.tensor_copy(best_id[:], best_at[:, :, 0:TOP])
                link(nc.vector.tensor_tensor(pair_sum[:], best[:, :, 0], best[:, :, 1], ALU.add))
                link(nc.vector.tensor_scalar(pair_inv[:], pair_sum[:], GUARD, None, ALU.max))
                link(nc.vector.reciprocal(pair_sum[:], pair_inv[:]))
                nc.vector.tensor_tensor(pair_w[:], best[:, :, 0:TOP], pair_sum[:].unsqueeze(2).to_broadcast([P, B, TOP]),
                                        ALU.mult)
                link(nc.vector.tensor_tensor(
                    chosen[:], expert_id[:].unsqueeze(1).unsqueeze(1).to_broadcast([P, B, TOP, E]),
                    best_id[:].unsqueeze(3).to_broadcast([P, B, TOP, E]), ALU.is_equal))
                link(nc.vector.tensor_tensor(weighed[:], chosen[:], pair_w[:].unsqueeze(3).to_broadcast([P, B, TOP, E]),
                                             ALU.mult))
                if not (isinstance(c, int) and c == 0):
                    dve.wait_ge(ct_product, c)
                link(nc.vector.tensor_tensor(combine[:, :, 0, :], weighed[:, :, 0, :], weighed[:, :, 1, :], ALU.add))
                for part in (1, 3):
                    last = nc.vector.tensor_copy(combine[:, :, part, :].bitcast(f32r), combine[:, :, 0, :])
                link(last)
                assert links[0] == SOFTMAX_LINKS
                nc.vector.tensor_tensor(combine[:, :, 2, :], combine[:, :, 0, :], combine[:, :, 1, :],
                                        ALU.subtract).then_inc(combine_done, 1)

            def step(s, parity, graph, next_group, select, experts):
                c, m = s - 1, s - 2
                if select:
                    links = shift_logits(c)
                if graph:
                    for k in range(C1):
                        round_off(ah_lo[:, k, :], pair_ps[k][:], ah_hi[:, k, :], ah_hi_ready, s * C1 + k + 1, ah_lo_ready)
                if experts:
                    gate_expert(m, parity, 0)
                    gate_expert(m, parity, 1)
                    gate_low(m, 0)
                if next_group:
                    first_moments(s + 1, 1 - parity)
                if experts:
                    gate_expert(m, parity, 2)
                    gate_low(m, 1)
                if select:
                    select_experts(c, links)
                if experts:
                    gate_expert(m, parity, 3)
                    gate_low(m, 2)
                if next_group:
                    first_norm(s + 1, 1 - parity)
                if experts:
                    gate_expert(m, parity, 4)
                    gate_low(m, 3)
                    gate_expert(m, parity, 5)
                if graph:
                    dve.wait_ge(as3_product, s + 1)
                    if not (isinstance(s, int) and s == 0):
                        dve.wait_ge(base_done, s)
                    nc.vector.tensor_tensor(x1[:].rearrange("p b f -> p (b f)"), chain_ps[:],
                                            x_sb[parity][:].rearrange("p b f -> p (b f)"), ALU.add).then_inc(x1_done, 1)
                    dve.wait_ge(x1_done, s + 1)
                    norm_moments(x1, stats2, moments2, moments2_done)
                if experts:
                    gate_low(m, 4)
                if next_group:
                    round_off(ax_lo[:], chain_ps[:], ax_hi[:], ax_hi_ready, s + 2, ax_lo_ready)
                if experts:
                    gate_expert(m, parity, 6)
                if graph:
                    normalise(x1, moments2, rstd2, rstd2_done, xhat2, xhat2_done, s)
                if experts:
                    gate_low(m, 5)
                    gate_expert(m, parity, 7)
                    gate_low(m, 6)
                    gate_low(m, 7)
                if graph:
                    round_off(xt_lo[parity][:], turn_ps[:], xt_hi[parity][:], xt_hi_ready, s + 1, xt_lo_ready)
                if experts:
                    dve.wait_ge(y_product, m + 1)
                    dve.wait_ge(base_done, m + 1)
                    if not (isinstance(m, int) and m < 2):
                        dve.wait_ge(out_stored[parity], (m - parity) * (DONE // 2))
                    nc.vector.tensor_tensor(out_sb[parity][:].rearrange("p b f -> p (b f)"), turn_ps[:],
                                            base[parity][:].rearrange("p b f -> p (b f)"), ALU.add).then_inc(out_ready, 1)

            def split(raw, hi, lo, hi_done, lo_done):
                nc.vector.tensor_copy(hi[:], raw[:]).then_inc(hi_done, 1)
                round_off(lo[:], raw[:], hi[:], hi_done, 1, lo_done)

            dve.wait_ge(graph_loaded, DONE)
            nc.vector.tensor_tensor(a_t[:], adj_sb[:], adj_sb[:], ALU.mult).then_inc(a_ready, 1)
            first_moments(0, 0)
            dve.wait_ge(w1_loaded, DONE)
            split(w1_raw, w1_hi, w1_lo, w1_split_hi, w1_split)
            first_norm(0, 0)
            dve.wait_ge(w2_loaded, DONE)
            split(w2_raw, w2_hi, w2_lo, w2_split_hi, w2_split)
            dve.wait_ge(router_loaded, DONE)
            nc.vector.tensor_copy(router[:, 0, :], router_raw[:]).then_inc(router_split_hi, 1)
            round_off(router[:, 1, :], router_raw[:], router[:, 0, :], router_split_hi, 1, router_split)
            dve.wait_ge(b2_loaded, (PARTS - 1) * DONE)
            split(b2_raw, b2_parts, b2_lo, b2_split_hi, b2_split)
            round_off(ax_lo[:], chain_ps[:], ax_hi[:], ax_hi_ready, 1, ax_lo_ready)
            dve.wait_ge(up_loaded, DONE)
            nc.vector.tensor_copy(up_hi[:], up_raw[:])
            dve.wait_ge(down_loaded, DONE)
            nc.vector.tensor_copy(down_hi[:], down_raw[:]).then_inc(ffn_split_hi, 1)
            dve.wait_ge(ffn_split_hi, 1)
            nc.vector.tensor_tensor(up_lo[:], up_raw[:], up_hi[:].bitcast(f32), ALU.subtract)
            nc.vector.tensor_tensor(down_lo[:], down_raw[:], down_hi[:].bitcast(f32), ALU.subtract).then_inc(ffn_split, 1)
            dve.wait_ge(consts_ready, 1)
            run_steps(dve, step)

        @block.scalar
        def _(act):
            def expert_hidden(m, e):
                act.wait_ge(hid_product, m * E + e + 1)
                if e >= HID_BUFS:
                    act.wait_ge(gated_ready, m * E + e - HID_BUFS + 1)
                nc.scalar.activation(hid[e % HID_BUFS][:], hid_ps[e % 2][:], ACT.Gelu,
                                     bias=b1_sb[:, e:e + 1]).then_inc(hid_ready, 1)

            def expert_high(m, e):
                act.wait_ge(gated_ready, m * E + e + 1)
                nc.scalar.activation(gated_hi[e][:], gated[e % GATED_BUFS][:], ACT.Copy).then_inc(gated_hi_ready, 1)

            def graph_head(group):
                act.wait_ge(ax_product, group + 1)
                nc.scalar.activation(ax_hi[:], chain_ps[:], ACT.Copy).then_inc(ax_hi_ready, 1)

            def graph_hidden1(group):
                for k in range(2):
                    act.wait_ge(h1_product, group * 2 + k + 1)
                    nc.scalar.activation(h1[:, 2 * k:2 * k + 2, :].rearrange("p b h -> p (b h)"), pair_ps[k][:],
                                         ACT.Relu).then_inc(h1_ready, 1)

            def combine_out(c):
                act.wait_ge(ct_product, c + 1)
                if not (isinstance(c, int) and c == 0):
                    act.wait_ge(ct_stored, c * DONE)
                nc.scalar.activation(ct_sb[:], route_ps[0:E, :], ACT.Copy)
                nc.scalar.activation(ct_parts[:], route_ps[0:PARTS * E, :], ACT.Copy).then_inc(ct_ready, 1)

            def step(s, parity, graph, next_group, select, experts):
                c, m = s - 1, s - 2
                if graph:
                    for k in range(C1):
                        act.wait_ge(ah_product, s * C1 + k + 1)
                        nc.scalar.activation(ah_hi[:, k, :], pair_ps[k][:], ACT.Copy).then_inc(ah_hi_ready, 1)
                if experts:
                    expert_hidden(m, 0)
                    expert_hidden(m, 1)
                for j in range(C2):
                    if graph:
                        act.wait_ge(h2_product, s * C2 + j + 1)
                        nc.scalar.activation(h2_t[:, j, :], pair_ps[j % 2][:], ACT.Relu).then_inc(h2_ready, 1)
                    if experts:
                        expert_high(m, j)
                        if j + 2 < 6:
                            expert_hidden(m, j + 2)
                if graph:
                    act.wait_ge(s3_product, s + 1)
                    nc.scalar.activation(s3[:].rearrange("p b f -> p (b f)"), chain_ps[:], ACT.Copy).then_inc(s3_ready, 1)
                if experts:
                    expert_high(m, 4)
                    expert_hidden(m, 6)
                if select and graph:
                    combine_out(c)
                if experts:
                    expert_high(m, 5)
                    expert_hidden(m, 7)
                if next_group:
                    graph_head(s + 1)
                if experts:
                    expert_high(m, 6)
                    expert_high(m, 7)
                if next_group:
                    graph_hidden1(s + 1)
                if select and not graph:
                    combine_out(c)
                if graph:
                    act.wait_ge(xt_product, s + 1)
                    nc.scalar.activation(xt_hi[parity][:], turn_ps[:], ACT.Copy).then_inc(xt_hi_ready, 1)
                if experts:
                    act.wait_ge(down_done, m + 1)
                    nc.scalar.activation(yt_sb[:], yt_ps[:], ACT.Copy).then_inc(yt_ready, 1)

            graph_head(0)
            graph_hidden1(0)
            act.wait_ge(b1_loaded, DONE)
            run_steps(act, step)

        @block.tensor
        def _(pe):
            def three_passes(dst, w_hi, w_lo, v_hi, v_lo, start, stop):
                nc.tensor.matmul(dst, w_hi, v_hi, start=start, stop=False)
                nc.tensor.matmul(dst, w_hi, v_lo, start=False, stop=False)
                return nc.tensor.matmul(dst, w_lo, v_hi, start=False, stop=stop)

            def expert_up(m, parity, e):
                if e >= 2:
                    pe.wait_ge(hid_ready, m * E + e - 1)
                three_passes(hid_ps[e % 2][:], up_hi[:, e, :], up_lo[:, e, :], xt_hi[parity][:], xt_lo[parity][:],
                             True, True).then_inc(hid_product, 1)

            def expert_down(m, e):
                pe.wait_ge(gated_lo_ready, m * E + e + 1)
                last = three_passes(yt_ps[:], down_hi[:, e, :], down_lo[:, e, :], gated_hi[e][:], gated_lo[e][:],
                                    False, e == E - 1)
                if e == E - 1:
                    last.then_inc(down_done, 1)

            def graph_ax(group):
                pe.wait_ge(xhat1_done, group + 1)
                if not (isinstance(group, int) and group == 0):
                    pe.wait_ge(x1_done, group)
                for b in range(B):
                    last = nc.tensor.matmul(chain_ps[:, b * P:(b + 1) * P], xhat1[:, b, :], a_t[:], start=True, stop=True)
                last.then_inc(ax_product, 1)

            def graph_hidden1(group):
                pe.wait_ge(ax_lo_ready, group + 1)
                for b in range(B):
                    dst = pair_ps[b // 2][:, (b % 2) * H1:(b % 2 + 1) * H1]
                    hi, lo = ax_hi[:, b * P:(b + 1) * P], ax_lo[:, b * P:(b + 1) * P]
                    nc.tensor.matmul(dst, hi, w1_hi[:], start=True, stop=False)
                    nc.tensor.matmul(dst, hi, w1_lo[:], start=False, stop=False)
                    last = nc.tensor.matmul(dst, lo, w1_hi[:], start=False, stop=True)
                    if b % 2:
                        last.then_inc(h1_product, 1)

            def graph_hidden2(s, j):
                if j == 0:
                    pe.wait_ge(ah_lo_ready, (s + 1) * C1)
                if j >= 2:
                    pe.wait_ge(h2_ready, s * C2 + j - 1)
                for k in range(C1):
                    last = three_passes(pair_ps[j % 2][:], w2_hi[:, k, j * P:(j + 1) * P], w2_lo[:, k, j * P:(j + 1) * P],
                                        ah_hi[:, k, :], ah_lo[:, k, :], k == 0, k == C1 - 1)
                last.then_inc(h2_product, 1)

            def graph_out(s, j):
                pe.wait_ge(h2_ready, s * C2 + j + 1)
                for b in range(B):
                    last = nc.tensor.matmul(chain_ps[:, b * F:(b + 1) * F], h2_t[:, j, b * P:(b + 1) * P], w3g[:, j, :],
                                            start=(j == 0 and b == 0), stop=(j == C2 - 1), skip_group_check=True)
                return last

            def combine_across(c):
                pe.wait_ge(combine_done, c + 1)
                for b in range(B):
                    last = nc.tensor.transpose(route_ps[0:PARTS * E, b * P:(b + 1) * P],
                                               combine[:, b, :, :].rearrange("p k e -> p (k e)"), ident[:])
                last.then_inc(ct_product, 1)

            def step(s, parity, graph, next_group, select, experts):
                c, m = s - 1, s - 2
                if graph:
                    pe.wait_ge(h1_ready, (s + 1) * 2)
                    for k in range(C1):
                        for b in range(B):
                            last = nc.tensor.matmul(pair_ps[k][:, b * P:(b + 1) * P], h1[:, b, k * P:(k + 1) * P], a_t[:],
                                                    start=True, stop=True)
                        last.then_inc(ah_product, 1)
                if experts:
                    expert_up(m, parity, 0)
                    expert_up(m, parity, 1)
                    nc.tensor.matmul(yt_ps[:], b2_parts[:], ct_parts[:], start=True, stop=False)
                if graph:
                    graph_hidden2(s, 0)
                for j in range(1, C2):
                    if graph:
                        graph_hidden2(s, j)
                    if experts:
                        expert_up(m, parity, j + 1)
                    if graph:
                        graph_out(s, j - 1)
                if experts:
                    expert_up(m, parity, 5)
                if graph:
                    graph_out(s, C2 - 1).then_inc(s3_product, 1)
                if select and graph:
                    combine_across(c)
                if experts:
                    expert_up(m, parity, 6)
                if graph:
                    pe.wait_ge(s3_ready, s + 1)
                    nc.tensor.matmul(chain_ps[:], a_t[:], s3[:].rearrange("p b f -> p (b f)"), start=True,
                                     stop=True).then_inc(as3_product, 1)
                if experts:
                    expert_up(m, parity, 7)
                    expert_down(m, 0)
                if next_group:
                    graph_ax(s + 1)
                if experts:
                    expert_down(m, 1)
                    expert_down(m, 2)
                if next_group:
                    graph_hidden1(s + 1)
                if experts:
                    expert_down(m, 3)
                    expert_down(m, 4)
                if graph:
                    pe.wait_ge(xhat2_done, s + 1)
                    for b in range(B):
                        last = nc.tensor.transpose(turn_ps[:, b * P:(b + 1) * P], xhat2[:, b, :], ident[:])
                    last.then_inc(xt_product, 1)
                if experts:
                    for e in range(5, E):
                        expert_down(m, e)
                if select and not graph:
                    combine_across(c)
                if graph:
                    pe.wait_ge(xt_lo_ready, s + 1)
                    if select:
                        pe.wait_ge(ct_ready, s)
                    weights = router[:].rearrange("p k e -> p (k e)")
                    for b in range(B):
                        dst = route_ps[:, b * 2 * E:(b + 1) * 2 * E]
                        nc.tensor.matmul(dst, xt_hi[parity][:, b * P:(b + 1) * P], weights, start=True, stop=False)
                        last = nc.tensor.matmul(dst, xt_lo[parity][:, b * P:(b + 1) * P], weights, start=False, stop=True)
                    last.then_inc(logits_product, 1)
                if experts:
                    pe.wait_ge(yt_ready, m + 1)
                    for b in range(B):
                        last = nc.tensor.transpose(turn_ps[:, b * F:(b + 1) * F], yt_sb[:, b * P:(b + 1) * P], ident[:])
                    last.then_inc(y_product, 1)

            pe.wait_ge(a_ready, 1)
            graph_ax(0)
            pe.wait_ge(w1_split, 1)
            graph_hidden1(0)
            pe.wait_ge(w2_split, 1)
            pe.wait_ge(w3_loaded, DONE)
            pe.wait_ge(consts_ready, 1)
            pe.wait_ge(router_split, 1)
            pe.wait_ge(b2_stacked, DONE)
            pe.wait_ge(ffn_split, 1)
            run_steps(pe, step)


_OUT = "out_dram"


def kernel(x, adj, L0_gnn_W1, L0_gnn_W2, L0_gnn_W3, L0_ffn_router_w, L0_ffn_w1, L0_ffn_b1, L0_ffn_w2, L0_ffn_b2):
    import numpy as np
    import concourse.bacc as bacc
    from concourse import mybir as mb
    from concourse.bass_utils import run_bass_kernel_spmd

    batches, nodes, features = x.shape
    per_group = 4
    groups = batches // per_group

    def grouped(a):
        return a.reshape(groups, per_group, nodes, features).transpose(0, 2, 1, 3).reshape(groups, nodes, -1)

    laid_out = {
        "x": grouped(np.asarray(x)),
        "adj_t": np.asarray(adj).T,
        "gnn_w1": np.asarray(L0_gnn_W1),
        "gnn_w2": np.asarray(L0_gnn_W2),
        "gnn_w3": np.asarray(L0_gnn_W3),
        "router_t": np.asarray(L0_ffn_router_w).T,
        "ffn_w1": np.asarray(L0_ffn_w1).transpose(1, 0, 2),
        "ffn_b1_t": np.asarray(L0_ffn_b1).T,
        "ffn_w2": np.asarray(L0_ffn_w2).transpose(1, 0, 2),
        "ffn_b2": np.asarray(L0_ffn_b2),
    }
    nc = bacc.Bacc("TRN2", target_bir_lowering=False, num_devices=1)
    arrays, args = {}, []
    for name, a in laid_out.items():
        a = np.ascontiguousarray(a)
        arrays[f"in_{name}"] = a
        args.append(nc.dram_tensor(f"in_{name}", a.shape, mb.dt.from_np(a.dtype), kind="ExternalInput").ap())
    out = nc.dram_tensor(_OUT, (groups, nodes, per_group * features), mb.dt.float32, kind="ExternalOutput").ap()
    gnn_moe_kernel(nc, *args, out)
    result = run_bass_kernel_spmd(nc, [arrays], core_ids=[0]).results[0][_OUT]
    return (result.reshape(groups, nodes, per_group, features).transpose(0, 2, 1, 3)
            .reshape(batches, nodes, features))
```

```python
import concourse.bass as bass
from concourse import mybir
from concourse.alu_op_type import AluOpType as ALU
from contextlib import ExitStack


def gnn_moe_kernel(
    nc: bass.Bass,
    x: bass.AP,
    adj_t: bass.AP,
    gnn_w1: bass.AP,
    gnn_w2: bass.AP,
    gnn_w3: bass.AP,
    router_t: bass.AP,
    ffn_w1: bass.AP,
    ffn_b1_t: bass.AP,
    ffn_w2: bass.AP,
    ffn_b2: bass.AP,
    out: bass.AP,
):
    f32 = mybir.dt.float32
    f32r = mybir.dt.float32r
    u32 = mybir.dt.uint32
    ACT = mybir.ActivationFunctionType
    AX = mybir.AxisListType.X

    GROUPS, P, GF = x.shape
    F = gnn_w1.shape[0]
    B = GF // F
    T = B * P
    H1 = gnn_w1.shape[1]
    H2 = gnn_w2.shape[1]
    C1 = H1 // P
    C2 = H2 // P
    E = ffn_w1.shape[1]
    TOP = 2
    BANK = 512
    BN = 6
    EPS = 1e-5
    GUARD = 1e-12
    DONE = 16
    GATED_BUFS = 4
    POOL_LOWS = (4, 5)
    GATE_PIECES = 4
    WAKING = 12
    PARTS = 4
    LOOP_FROM, LOOP_TO = 4, GROUPS - 2

    ctx = ExitStack()
    with ctx:
        def sb(name, shape, dt=f32):
            return ctx.enter_context(nc.sbuf_tensor(name, shape, dt))

        def pb(name):
            return ctx.enter_context(nc.psum_tensor(name, [P, BANK], f32))

        def sem(name):
            return ctx.enter_context(nc.semaphore(name))

        ident = sb("ident", [P, P])
        expert_id = sb("expert_id", [P, E])
        neg_half = sb("neg_half", [P, B])
        neg_one = sb("neg_one", [P, B])
        eps = sb("eps", [P, B])
        euler = sb("euler", [P, B * E])
        adj_sb = sb("adj_sb", [P, P])
        a_t = sb("a_t", [P, P])
        a_hi = sb("a_hi", [P, P], f32r)
        a_lo = sb("a_lo", [P, P], f32r)
        w1_raw = sb("w1_raw", [P, H1])
        w1_hi = sb("w1_hi", [P, H1], f32r)
        w1_lo = sb("w1_lo", [P, H1], f32r)
        w2_raw = sb("w2_raw", [P, C1, H2])
        w2_hi = sb("w2_hi", [P, C1, H2], f32r)
        w2_lo = sb("w2_lo", [P, C1, H2], f32r)
        w3_sb = sb("w3_sb", [P, C2, F])
        up_raw = sb("up_raw", [P, E, P])
        up_hi = sb("up_hi", [P, E, P], f32r)
        up_lo = sb("up_lo", [P, E, P], f32r)
        down_raw = sb("down_raw", [P, E, F])
        down_hi = sb("down_hi", [P, E, F], f32r)
        down_lo = sb("down_lo", [P, E, F], f32r)
        b1_sb = sb("b1_sb", [P, E])
        b2_raw = sb("b2_raw", [PARTS * E, F])
        b2_lo = sb("b2_lo", [PARTS * E, F], f32r)
        b2_parts = sb("b2_parts", [PARTS * E, F], f32r)
        router = sb("router", [P, E])

        x_sb = [sb(f"x_sb{i}", [P, B, F]) for i in range(2)]
        xhat1 = sb("xhat1", [P, B, F])
        stats1 = sb("stats1", [P, B, BN])
        moments1 = sb("moments1", [P, B, 2])
        var1 = sb("var1", [P, B])
        rstd1 = sb("rstd1", [P, B])
        neg_mean = sb("neg_mean", [P, B])
        offset1 = sb("offset1", [P, B])
        ax_hi = sb("ax_hi", [P, T], f32r)
        ax_lo = sb("ax_lo", [P, T], f32r)
        h1 = sb("h1", [P, B, H1])
        ah_hi = sb("ah_hi", [P, C1, T], f32r)
        ah_lo = sb("ah_lo", [P, C1, T], f32r)
        h2_t = sb("h2_t", [P, C2, T])
        s3_hi = sb("s3_hi", [P, B * F], f32r)
        s3_lo = sb("s3_lo", [P, B * F], f32r)
        x1 = sb("x1", [P, B, F])
        xhat2 = sb("xhat2", [P, B, F])
        stats2 = sb("stats2", [P, B, BN])
        moments2 = sb("moments2", [P, B, 2])
        var2 = sb("var2", [P, B])
        rstd2 = sb("rstd2", [P, B])
        base = [sb(f"base{i}", [P, B, F]) for i in range(2)]
        xt = sb("xt", [P, T])
        xt_hi = [sb(f"xt_hi{i}", [P, T], f32r) for i in range(2)]
        xt_lo = [sb(f"xt_lo{i}", [P, T], f32r) for i in range(2)]
        top_logit = sb("top_logit", [P, B])
        shifted = sb("shifted", [P, B, E])
        exps = sb("exps", [P, B, E])
        exp_sum = sb("exp_sum", [P, B])
        exp_inv = sb("exp_inv", [P, B])
        probs = sb("probs", [P, B, E])
        best = sb("best", [P, B, 8])
        best_at = sb("best_at", [P, B, 8], u32)
        best_id = sb("best_id", [P, B, TOP])
        pair_sum = sb("pair_sum", [P, B])
        pair_inv = sb("pair_inv", [P, B])
        pair_w = sb("pair_w", [P, B, TOP])
        chosen = sb("chosen", [P, B, TOP, E])
        weighed = sb("weighed", [P, B, TOP, E])
        combine = sb("combine", [P, B, PARTS, E])
        ct_sb = sb("ct_sb", [E, T])
        ct_parts = sb("ct_parts", [PARTS * E, T], f32r)
        gate = [sb(f"gate{i}", [P, E, T]) for i in range(2)]
        hid = [sb(f"hid{i}", [P, T]) for i in range(E)]
        gated = [sb(f"gated{i}", [P, T]) for i in range(GATED_BUFS)]
        gated_hi = [sb(f"gated_hi{i}", [P, T], f32r) for i in range(E)]
        gated_lo = [sb(f"gated_lo{i}", [P, T], f32r) for i in range(E)]
        yt_sb = sb("yt_sb", [P, T])
        out_sb = [sb(f"out_sb{i}", [P, B, F]) for i in range(2)]
        ct_dram = nc.dram_tensor("ct_dram", [GROUPS, E, T], f32, kind="Internal").ap()

        chain_ps = pb("chain_ps")
        pair_ps = [pb(f"pair_ps{i}") for i in range(2)]
        turn_ps = pb("turn_ps")
        route_ps = pb("route_ps")
        hid_ps = [pb(f"hid_ps{i}") for i in range(2)]
        yt_ps = pb("yt_ps")
        all_hid_ps = hid_ps + pair_ps
        final_ps = chain_ps
        early_ps = yt_ps

        graph_loaded = sem("graph_loaded")
        w1_loaded = sem("w1_loaded")
        w2_loaded = sem("w2_loaded")
        w3_loaded = sem("w3_loaded")
        router_loaded = sem("router_loaded")
        b1_loaded = sem("b1_loaded")
        b2_loaded = sem("b2_loaded")
        up_loaded = sem("up_loaded")
        down_loaded = sem("down_loaded")
        x_loaded = [sem(f"x_loaded{i}") for i in range(2)]
        ct_stored = sem("ct_stored")
        gate_loaded = [[sem(f"gate_loaded{i}{piece}") for piece in range(GATE_PIECES)] for i in range(2)]
        out_stored = [sem(f"out_stored{i}") for i in range(2)]
        ident_zero = sem("ident_zero")
        consts_ready = sem("consts_ready")
        ids_int = sem("ids_int")
        a_ready = sem("a_ready")
        a_split_hi = sem("a_split_hi")
        a_split = sem("a_split")
        w1_split_hi = sem("w1_split_hi")
        w1_split = sem("w1_split")
        w2_split_hi = sem("w2_split_hi")
        w2_split = sem("w2_split")
        b2_zero = sem("b2_zero")
        b2_split_hi = sem("b2_split_hi")
        b2_split = sem("b2_split")
        b2_stacked = sem("b2_stacked")
        up_split_hi = sem("up_split_hi")
        up_split = sem("up_split")
        down_split_hi = sem("down_split_hi")
        down_split = sem("down_split")
        moments1_done = sem("moments1_done")
        var1_done = sem("var1_done")
        rstd1_done = sem("rstd1_done")
        neg_mean_done = sem("neg_mean_done")
        offset1_done = sem("offset1_done")
        xhat1_done = sem("xhat1_done")
        ax_product = sem("ax_product")
        ax_hi_ready = sem("ax_hi_ready")
        ax_lo_ready = sem("ax_lo_ready")
        h1_product = sem("h1_product")
        h1_ready = sem("h1_ready")
        ah_product = sem("ah_product")
        ah_hi_ready = sem("ah_hi_ready")
        ah_lo_ready = sem("ah_lo_ready")
        h2_product = sem("h2_product")
        h2_ready = sem("h2_ready")
        s3_product = sem("s3_product")
        s3_hi_ready = sem("s3_hi_ready")
        s3_lo_ready = sem("s3_lo_ready")
        as3_product = sem("as3_product")
        x1_done = sem("x1_done")
        moments2_done = sem("moments2_done")
        var2_done = sem("var2_done")
        rstd2_done = sem("rstd2_done")
        xhat2_done = sem("xhat2_done")
        base_done = sem("base_done")
        xt_product = sem("xt_product")
        xt_ready = sem("xt_ready")
        xt_hi_ready = sem("xt_hi_ready")
        xt_lo_ready = sem("xt_lo_ready")
        logits_product = sem("logits_product")
        softmax_link = sem("softmax_link")
        shifted_done = sem("shifted_done")
        exps_done = sem("exps_done")
        combine_done = sem("combine_done")
        ct_product = sem("ct_product")
        ct_sb_ready = sem("ct_sb_ready")
        ct_ready = sem("ct_ready")
        hid_product = sem("hid_product")
        hid_ready = sem("hid_ready")
        gated_ready = sem("gated_ready")
        gated_hi_ready = sem("gated_hi_ready")
        gated_lo_ready = sem("gated_lo_ready")
        gated_lo_pool_ready = sem("gated_lo_pool_ready")
        down_done = sem("down_done")
        final_down = sem("final_down")
        yt_ready = sem("yt_ready")
        y_product = sem("y_product")
        out_ready = sem("out_ready")

        SOFTMAX_LINKS = 13

        def run_steps(eng, step):
            everything = dict(graph=True, next_group=True, load_ahead=True, select=True, experts=True)
            step(0, 0, **{**everything, "select": False, "experts": False})
            step(1, 1, **{**everything, "experts": False})
            step(2, 0, **everything)
            step(3, 1, **everything)
            with eng.Fori(LOOP_FROM // 2, LOOP_TO // 2, 1) as pair:
                for parity in range(2):
                    step(pair * 2 + parity, parity, **everything)
            step(LOOP_TO, 0, **{**everything, "load_ahead": False})
            step(LOOP_TO + 1, 1, **{**everything, "load_ahead": False, "next_group": False})
            step(GROUPS, 0, graph=False, next_group=False, load_ahead=False, select=True, experts=True)
            step(GROUPS + 1, 1, graph=False, next_group=False, load_ahead=False, select=False, experts=True)

        def lows_before(m, e):
            return m * (E - len(POOL_LOWS)) + sum(i not in POOL_LOWS for i in range(e + 1))

        def first_step(s):
            return isinstance(s, int) and s == 0

        def turns_late(s):
            return isinstance(s, int) and s < 3

        def ah_ahead(s):
            return isinstance(s, int) and 0 < s < 3

        def landed(group, parity):
            return (group - parity) * (DONE // 2) + DONE

        block = ctx.enter_context(nc.Block())

        @block.sync
        def _(sp):
            sp.dma_start(x_sb[0][:], x[0].rearrange("p (b f) -> p b f", b=B)).then_inc(x_loaded[0], DONE)
            sp.dma_start(adj_sb[:], adj_t).then_inc(graph_loaded, DONE)
            sp.dma_start(w1_raw[:], gnn_w1).then_inc(w1_loaded, DONE)
            sp.dma_start(w2_raw[:], gnn_w2.rearrange("(c p) h -> p c h", p=P)).then_inc(w2_loaded, DONE)
            sp.dma_start(x_sb[1][:], x[1].rearrange("p (b f) -> p b f", b=B)).then_inc(x_loaded[1], DONE)
            sp.dma_start(w3_sb[:], gnn_w3.rearrange("(c p) f -> p c f", p=P)).then_inc(w3_loaded, DONE)
            sp.dma_start(router[:], router_t).then_inc(router_loaded, DONE)
            sp.dma_start(b1_sb[:], ffn_b1_t).then_inc(b1_loaded, DONE)
            sp.wait_ge(b2_zero, 1)
            for part in range(1, PARTS):
                sp.dma_start(b2_raw[part * E:(part + 1) * E, :], ffn_b2).then_inc(b2_loaded, DONE)
            sp.dma_start(up_raw[:], ffn_w1).then_inc(up_loaded, DONE)
            sp.dma_start(down_raw[:], ffn_w2).then_inc(down_loaded, DONE)
            sp.wait_ge(b2_split, 1)
            last_rows = slice((PARTS - 1) * E, PARTS * E)
            sp.dma_start(b2_parts[last_rows, :].bitcast(f32),
                         b2_lo[last_rows, :].bitcast(f32)).then_inc(b2_stacked, DONE)

            def step(s, parity, graph, next_group, load_ahead, select, experts):
                c, m = s - 1, s - 2
                if load_ahead:
                    x_from = x[bass.ds(s + 2, 1)].rearrange("o p (b f) -> (o p) b f", b=B)
                    sp.wait_ge(x1_done, s + 1)
                    sp.dma_start(x_sb[parity][:], x_from).then_inc(x_loaded[parity], DONE)
                if select:
                    ct_to = ct_dram[bass.ds(c, 1)].rearrange("o e t -> (o e) t")
                    gate_from = (ct_dram[bass.ds(c, 1)].rearrange("o e t -> o (e t)").partition_broadcast(P)
                                 .rearrange("p o (h e t) -> p (o h) e t", h=GATE_PIECES, e=E // GATE_PIECES))
                    if not (isinstance(s, int) and s < 3):
                        sp.wait_ge(yt_ready, c - 1)
                    sp.wait_ge(ct_sb_ready, c + 1)
                    sp.dma_start(ct_to, ct_sb[:]).then_inc(ct_stored, DONE)
                    sp.wait_ge(ct_stored, (c + 1) * DONE)
                    for piece in range(GATE_PIECES):
                        some = slice(piece * E // GATE_PIECES, (piece + 1) * E // GATE_PIECES)
                        sp.dma_start(gate[1 - parity][:, some, :],
                                     gate_from[:, piece, :, :]).then_inc(gate_loaded[1 - parity][piece], DONE)
                if experts:
                    out_to = out[bass.ds(m, 1)].rearrange("o p (b f) -> (o p) b f", b=B)
                    sp.wait_ge(out_ready, m + 1)
                    sp.dma_start(out_to, out_sb[parity][:]).then_inc(out_stored[parity], DONE)

            run_steps(sp, step)
            for parity in range(2):
                sp.wait_ge(out_stored[parity], GROUPS // 2 * DONE)

        @block.gpsimd
        def _(pool):
            nc.gpsimd.memset(b2_raw[:], 0.0).then_inc(b2_zero, 1)
            nc.gpsimd.memset(ident[:], 0.0).then_inc(ident_zero, 1)
            nc.gpsimd.memset(neg_half[:], -0.5)
            nc.gpsimd.memset(neg_one[:], -1.0)
            nc.gpsimd.memset(eps[:], EPS)
            nc.gpsimd.memset(euler[:], 2.718281828459045)
            nc.gpsimd.iota(best_at[:, 0, 0:E], pattern=[[1, E]], base=0, channel_multiplier=0).then_inc(ids_int, 1)
            pool.wait_ge(ids_int, 1)
            nc.gpsimd.tensor_copy(expert_id[:], best_at[:, 0, 0:E])
            pool.wait_ge(ident_zero, 1)
            nc.gpsimd.affine_select(out=ident[:], in_=ident[:], compare_op=ALU.not_equal, fill=1.0, base=0,
                                    pattern=[[-1, P]], channel_multiplier=1).then_inc(consts_ready, 1)

            def root(group, moments_done, moments, var, var_done, rstd, rstd_done):
                pool.wait_ge(moments_done, group + 1)
                nc.gpsimd.tensor_tensor(var[:], moments[:, :, 1], eps[:], ALU.add).then_inc(var_done, 1)
                pool.wait_ge(var_done, group + 1)
                nc.gpsimd.tensor_tensor(rstd[:], var[:], neg_half[:], ALU.pow).then_inc(rstd_done, 1)

            def residual_late(group):
                return isinstance(group, int) and (group < 2 or group == GROUPS - 1)

            def residual(group, parity):
                pool.wait_ge(xhat2_done, group + 1)
                if not (isinstance(group, int) and group < 2):
                    pool.wait_ge(out_ready, group - 1)
                nc.gpsimd.tensor_tensor(base[parity][:], x1[:], xhat2[:], ALU.add).then_inc(base_done, 1)

            def first_scales(group):
                root(group, moments1_done, moments1, var1, var1_done, rstd1, rstd1_done)
                pool.wait_ge(rstd1_done, group + 1)
                nc.gpsimd.tensor_tensor(neg_mean[:], moments1[:, :, 0], neg_one[:], ALU.mult).then_inc(neg_mean_done, 1)
                pool.wait_ge(neg_mean_done, group)
                nc.gpsimd.tensor_tensor(offset1[:], neg_mean[:], rstd1[:], ALU.mult).then_inc(offset1_done, 1)

            def step(s, parity, graph, next_group, load_ahead, select, experts):
                c = s - 1
                if select:
                    pool.wait_ge(shifted_done, s)
                    nc.gpsimd.tensor_tensor(exps[:].rearrange("p b e -> p (b e)"), euler[:],
                                            shifted[:].rearrange("p b e -> p (b e)"), ALU.pow).then_inc(exps_done, 1)
                if select and residual_late(c):
                    residual(c, 1 - parity)
                if experts and (graph or select):
                    for e in POOL_LOWS:
                        pool.wait_ge(gated_hi_ready, (s - 2) * E + e + 1)
                        nc.gpsimd.tensor_tensor(gated_lo[e][:], gated[e % GATED_BUFS][:], gated_hi[e][:].bitcast(f32),
                                                ALU.subtract).then_inc(gated_lo_pool_ready, 1)
                if graph:
                    root(s, moments2_done, moments2, var2, var2_done, rstd2, rstd2_done)
                    if load_ahead:
                        first_scales(s + 2)
                    if not residual_late(s):
                        residual(s, parity)

            pool.wait_ge(consts_ready, 1)
            root(0, moments1_done, moments1, var1, var1_done, rstd1, rstd1_done)
            first_scales(1)
            run_steps(pool, step)

        @block.vector
        def _(dve):
            def norm_moments(v, stats, moments, moments_done):
                for b in range(B):
                    nc.vector.bn_stats(stats[:, b, :], v[:, b, :])
                dve.drain()
                for b in range(B):
                    last = nc.vector.bn_aggr(moments[:, b, :], stats[:, b, :])
                last.then_inc(moments_done, 1)

            def normalise(v, moments, rstd, rstd_done, xhat, xhat_done, group):
                dve.wait_ge(rstd_done, group + 1)
                for b in range(B):
                    last = nc.vector.tensor_scalar(xhat[:, b, :], v[:, b, :], moments[:, b, 0:1], rstd[:, b:b + 1],
                                                   ALU.subtract, ALU.mult)
                last.then_inc(xhat_done, 1)

            def first_moments(group, parity):
                dve.wait_ge(x_loaded[parity], landed(group, parity))
                norm_moments(x_sb[parity], stats1, moments1, moments1_done)

            def round_off(lo, value, hi, hi_ready, count, lo_ready):
                dve.wait_ge(hi_ready, count)
                nc.vector.tensor_tensor(lo, value, hi.bitcast(f32), ALU.subtract).then_inc(lo_ready, 1)

            def gate_expert(m, parity, e, final=False):
                dve.wait_ge(hid_ready, m * E + e + 1)
                if e % (E // GATE_PIECES) == 0:
                    dve.wait_ge(gate_loaded[parity][e // (E // GATE_PIECES)], landed(m, parity))
                if e == 0 and final:
                    dve.wait_ge(gated_lo_pool_ready, m * len(POOL_LOWS))
                if e >= GATED_BUFS and final:
                    dve.wait_ge(final_down, e - GATED_BUFS + 1)
                elif e >= GATED_BUFS:
                    dve.wait_ge(gated_lo_ready, lows_before(m, e - GATED_BUFS))
                nc.vector.tensor_tensor(gated[e % GATED_BUFS][:], hid[e][:], gate[parity][:, e, :],
                                        ALU.mult).then_inc(gated_ready, 1)

            def gate_low(m, e):
                round_off(gated_lo[e][:], gated[e % GATED_BUFS][:], gated_hi[e][:], gated_hi_ready, m * E + e + 1,
                          gated_lo_ready)

            def shift_logits(c):
                dve.wait_ge(logits_product, c + 1)
                logits = route_ps[:, 0:B * E].rearrange("p (b e) -> p b e", b=B)
                nc.vector.tensor_reduce(top_logit[:], logits, AX, ALU.max).then_inc(softmax_link, 1)
                dve.wait_ge(softmax_link, c * SOFTMAX_LINKS + 1)
                nc.vector.tensor_tensor(shifted[:], logits, top_logit[:].unsqueeze(2).to_broadcast([P, B, E]),
                                        ALU.subtract).then_inc(shifted_done, 1)

            def select_experts(c):
                links = [1]

                def link(instruction, alone=False):
                    links[0] += 1
                    instruction.then_inc(softmax_link, 1)
                    if alone:
                        dve.drain()
                        return
                    dve.wait_ge(softmax_link, c * SOFTMAX_LINKS + links[0])

                dve.wait_ge(exps_done, c + 1)
                link(nc.vector.tensor_reduce(exp_sum[:], exps[:], AX, ALU.add))
                link(nc.vector.reciprocal(exp_inv[:], exp_sum[:]))
                link(nc.vector.tensor_tensor(probs[:], exps[:], exp_inv[:].unsqueeze(2).to_broadcast([P, B, E]),
                                             ALU.mult), alone=True)
                for b in range(B):
                    last = nc.vector.max(best[:, b, :], probs[:, b, :])
                link(last, alone=True)
                for b in range(B):
                    last = nc.vector.max_index(best_at[:, b, :], best[:, b, :], probs[:, b, :])
                link(last)
                nc.vector.tensor_copy(best_id[:], best_at[:, :, 0:TOP])
                link(nc.vector.tensor_tensor(pair_sum[:], best[:, :, 0], best[:, :, 1], ALU.add))
                link(nc.vector.tensor_scalar(pair_inv[:], pair_sum[:], GUARD, None, ALU.max))
                link(nc.vector.reciprocal(pair_sum[:], pair_inv[:]))
                nc.vector.tensor_tensor(pair_w[:], best[:, :, 0:TOP],
                                        pair_sum[:].unsqueeze(2).to_broadcast([P, B, TOP]), ALU.mult)
                link(nc.vector.tensor_tensor(
                    chosen[:], expert_id[:].unsqueeze(1).unsqueeze(1).to_broadcast([P, B, TOP, E]),
                    best_id[:].unsqueeze(3).to_broadcast([P, B, TOP, E]), ALU.is_equal))
                link(nc.vector.tensor_tensor(weighed[:], chosen[:], pair_w[:].unsqueeze(3).to_broadcast([P, B, TOP, E]),
                                             ALU.mult))
                if not (isinstance(c, int) and c == 0):
                    dve.wait_ge(ct_product, c)
                link(nc.vector.tensor_tensor(combine[:, :, 0, :], weighed[:, :, 0, :], weighed[:, :, 1, :], ALU.add))
                for part in (1, 3):
                    last = nc.vector.tensor_copy(combine[:, :, part, :].bitcast(f32r), combine[:, :, 0, :])
                link(last)
                assert links[0] == SOFTMAX_LINKS
                nc.vector.tensor_tensor(combine[:, :, 2, :], combine[:, :, 0, :], combine[:, :, 1, :],
                                        ALU.subtract).then_inc(combine_done, 1)

            def head_low(group, bank):
                round_off(ax_lo[:], bank[:], ax_hi[:], ax_hi_ready, group + 1, ax_lo_ready)

            def ah_low(group):
                for k in range(C1):
                    round_off(ah_lo[:, k, :], pair_ps[k][:], ah_hi[:, k, :], ah_hi_ready, group * C1 + k + 1,
                              ah_lo_ready)

            def split(raw, hi, lo, hi_done, lo_done):
                nc.vector.tensor_copy(hi[:], raw[:]).then_inc(hi_done, 1)
                round_off(lo[:], raw[:], hi[:], hi_done, 1, lo_done)

            def split_later_weights():
                split(a_t, a_hi, a_lo, a_split_hi, a_split)
                dve.wait_ge(b2_loaded, (PARTS - 1) * DONE)
                split(b2_raw, b2_parts, b2_lo, b2_split_hi, b2_split)
                dve.wait_ge(up_loaded, DONE)
                split(up_raw, up_hi, up_lo, up_split_hi, up_split)
                dve.wait_ge(down_loaded, DONE)
                split(down_raw, down_hi, down_lo, down_split_hi, down_split)

            def s3_low(group):
                round_off(s3_lo[:], chain_ps[:], s3_hi[:], s3_hi_ready, group + 1, s3_lo_ready)

            def turned_low(group, parity):
                round_off(xt_lo[parity][:], turn_ps[:], xt_hi[parity][:], xt_hi_ready, group + 1, xt_lo_ready)

            def second_norm(s):
                normalise(x1, moments2, rstd2, rstd2_done, xhat2, xhat2_done, s)

            def write_out(m, parity, bank):
                dve.wait_ge(y_product, m + 1)
                dve.wait_ge(base_done, m + 1)
                if not (isinstance(m, int) and m < 2):
                    dve.wait_ge(out_stored[parity], (m - parity) * (DONE // 2))
                nc.vector.tensor_tensor(out_sb[parity][:].rearrange("p b f -> p (b f)"), bank[:],
                                        base[parity][:].rearrange("p b f -> p (b f)"), ALU.add).then_inc(out_ready, 1)

            def step(s, parity, graph, next_group, load_ahead, select, experts):
                c, m = s - 1, s - 2
                if graph:
                    if not ah_ahead(s):
                        ah_low(s)
                    if first_step(s):
                        split_later_weights()
                    if turns_late(s):
                        if select:
                            second_norm(c)
                            first_moments(s + 1, 1 - parity)
                            turned_low(c, 1 - parity)
                            shift_logits(c)
                        if s == 1:
                            head_low(2, early_ps)
                        if experts:
                            gate_expert(m, parity, 0)
                            gate_expert(m, parity, 1)
                            gate_low(m, 0)
                    else:
                        gate_expert(m, parity, 0)
                        gate_expert(m, parity, 1)
                        turned_low(c, 1 - parity)
                        gate_low(m, 0)
                        shift_logits(c)
                    if experts:
                        gate_expert(m, parity, 2)
                        gate_low(m, 1)
                        gate_expert(m, parity, 3)
                        gate_low(m, 2)
                        gate_expert(m, parity, 4)
                    if not experts:
                        s3_low(s)
                    if select:
                        select_experts(c)
                    if experts:
                        gate_low(m, 3)
                        s3_low(s)
                        gate_expert(m, parity, 5)
                        gate_expert(m, parity, 6)
                    else:
                        ah_low(s + 1)
                    dve.wait_ge(as3_product, s + 1)
                    if not first_step(s):
                        dve.wait_ge(base_done, s)
                    nc.vector.tensor_tensor(x1[:].rearrange("p b f -> p (b f)"), chain_ps[:],
                                            x_sb[parity][:].rearrange("p b f -> p (b f)"), ALU.add).then_inc(x1_done, 1)
                    dve.wait_ge(x1_done, s + 1)
                    norm_moments(x1, stats2, moments2, moments2_done)
                    if experts:
                        gate_expert(m, parity, 7)
                    if not next_group:
                        second_norm(s)
                    if experts:
                        gate_low(m, 6)
                        gate_low(m, 7)
                    if next_group and experts:
                        head_low(s + 1, chain_ps)
                        second_norm(s)
                        if load_ahead:
                            first_moments(s + 2, parity)
                    elif not next_group:
                        turned_low(s, parity)
                        shift_logits(s)
                elif select:
                    for e in range(4):
                        gate_expert(m, parity, e)
                    gate_low(m, 0)
                    gate_low(m, 1)
                    select_experts(c)
                    gate_low(m, 2)
                    gate_low(m, 3)
                    for e in range(4, E):
                        gate_expert(m, parity, e)
                    gate_low(m, 6)
                    gate_low(m, 7)
                else:
                    for e in range(E):
                        gate_expert(m, parity, e, final=True)
                        if e == 1:
                            write_out(m - 1, 1 - parity, turn_ps)
                if graph and experts:
                    write_out(m, parity, turn_ps)
                elif not graph and not select:
                    write_out(m, parity, final_ps)

            first_moments(0, 0)
            dve.wait_ge(graph_loaded, DONE)
            nc.vector.tensor_tensor(a_t[:], adj_sb[:], adj_sb[:], ALU.mult).then_inc(a_ready, 1)
            dve.wait_ge(w1_loaded, DONE)
            split(w1_raw, w1_hi, w1_lo, w1_split_hi, w1_split)
            normalise(x_sb[0], moments1, rstd1, rstd1_done, xhat1, xhat1_done, 0)
            first_moments(1, 1)
            head_low(0, chain_ps)
            dve.wait_ge(w2_loaded, DONE)
            split(w2_raw, w2_hi, w2_lo, w2_split_hi, w2_split)
            head_low(1, early_ps)
            dve.wait_ge(consts_ready, 1)
            run_steps(dve, step)

        @block.scalar
        def _(act):
            def expert_hidden(m, e, banks=hid_ps):
                act.wait_ge(hid_product, m * E + e + 1)
                nc.scalar.activation(hid[e][:], banks[e % len(banks)][:], ACT.Gelu,
                                     bias=b1_sb[:, e:e + 1]).then_inc(hid_ready, 1)

            def expert_high(m, e):
                act.wait_ge(gated_ready, m * E + e + 1)
                nc.scalar.activation(gated_hi[e][:], gated[e % GATED_BUFS][:], ACT.Copy).then_inc(gated_hi_ready, 1)

            def graph_head(group, bank):
                act.wait_ge(ax_product, group + 1)
                nc.scalar.activation(ax_hi[:], bank[:], ACT.Copy).then_inc(ax_hi_ready, 1)

            def graph_hidden1(group, k, banks):
                act.wait_ge(h1_product, group * 2 + k + 1)
                nc.scalar.activation(h1[:, 2 * k:2 * k + 2, :].rearrange("p b h -> p (b h)"), banks[k][:],
                                     ACT.Relu).then_inc(h1_ready, 1)

            def ah_high(group):
                for k in range(C1):
                    act.wait_ge(ah_product, group * C1 + k + 1)
                    nc.scalar.activation(ah_hi[:, k, :], pair_ps[k][:], ACT.Copy).then_inc(ah_hi_ready, 1)

            def turned_high(group, parity):
                act.wait_ge(xt_product, group + 1)
                nc.scalar.activation(xt[:], turn_ps[:], ACT.Copy).then_inc(xt_ready, 1)
                nc.scalar.activation(xt_hi[parity][:], turn_ps[:], ACT.Copy).then_inc(xt_hi_ready, 1)

            def first_norm(group, parity, half):
                act.wait_ge(offset1_done, group)
                for b in (2 * half, 2 * half + 1):
                    last = nc.scalar.activation(xhat1[:, b, :], x_sb[parity][:, b, :], ACT.Identity,
                                                bias=offset1[:, b:b + 1], scale=rstd1[:, b:b + 1])
                if half == 1:
                    last.then_inc(xhat1_done, 1)

            def combine_out(c):
                act.wait_ge(ct_product, c + 1)
                if not (isinstance(c, int) and c == 0):
                    act.wait_ge(ct_stored, c * DONE)
                nc.scalar.activation(ct_sb[:], route_ps[0:E, :], ACT.Copy).then_inc(ct_sb_ready, 1)
                nc.scalar.activation(ct_parts[:], route_ps[0:PARTS * E, :], ACT.Copy).then_inc(ct_ready, 1)

            def step(s, parity, graph, next_group, load_ahead, select, experts):
                c, m = s - 1, s - 2
                if graph:
                    if not ah_ahead(s):
                        ah_high(s)
                    if first_step(s):
                        graph_hidden1(1, 0, hid_ps)
                        graph_hidden1(1, 1, hid_ps)
                    if experts:
                        expert_hidden(m, 0)
                        expert_hidden(m, 1)
                    if not turns_late(s):
                        turned_high(c, 1 - parity)
                        expert_high(m, 0)
                    for j in range(C2):
                        act.wait_ge(h2_product, s * C2 + j + 1)
                        nc.scalar.activation(h2_t[:, j, :], pair_ps[j % 2][:], ACT.Relu).then_inc(h2_ready, 1)
                        if j == 1 and select and not experts:
                            turned_high(c, 1 - parity)
                        if j == 2 and select and not experts:
                            first_norm(2, 0, 0)
                            first_norm(2, 0, 1)
                        if j == 3 and select and not experts:
                            graph_head(2, early_ps)
                        if experts:
                            if j == 0:
                                expert_hidden(m, 2)
                            expert_hidden(m, j + 3)
                            if j == 0 and turns_late(s):
                                turned_high(c, 1 - parity)
                            if j == 1 and turns_late(s):
                                expert_high(m, 0)
                                expert_high(m, 1)
                            if j > 0 or not turns_late(s):
                                expert_high(m, j + 1)
                            if next_group and j in ((1, 3) if turns_late(s) else (1, 2)):
                                first_norm(s + 1, 1 - parity, j // 2)
                    act.wait_ge(s3_product, s + 1)
                    nc.scalar.activation(s3_hi[:], chain_ps[:], ACT.Copy).then_inc(s3_hi_ready, 1)
                    if not experts:
                        if select:
                            graph_hidden1(2, 0, hid_ps)
                            graph_hidden1(2, 1, hid_ps)
                        ah_high(s + 1)
                    if experts:
                        expert_hidden(m, 7)
                    if select:
                        combine_out(c)
                    if experts:
                        expert_high(m, 5)
                        expert_high(m, 6)
                    if next_group and experts:
                        graph_head(s + 1, chain_ps)
                    if experts:
                        expert_high(m, 7)
                    if not next_group:
                        turned_high(s, parity)
                elif select:
                    for e in range(E):
                        expert_hidden(m, e, all_hid_ps)
                        if e >= 3 and e < 7:
                            expert_high(m, e - 3)
                    for e in range(4):
                        expert_hidden(m + 1, e, all_hid_ps)
                    combine_out(c)
                    expert_high(m, 4)
                    expert_high(m, 5)
                    expert_high(m, 6)
                    expert_high(m, 7)
                    for e in range(4, 7):
                        expert_hidden(m + 1, e, all_hid_ps)
                else:
                    expert_hidden(m, 7, all_hid_ps)
                if experts and (graph or select):
                    act.wait_ge(down_done, m + 1)
                    nc.scalar.activation(yt_sb[:], yt_ps[:], ACT.Copy).then_inc(yt_ready, 1)
                if next_group and experts:
                    graph_hidden1(s + 1, 0, pair_ps)
                    graph_hidden1(s + 1, 1, pair_ps)

            graph_head(0, chain_ps)
            first_norm(1, 1, 0)
            first_norm(1, 1, 1)
            graph_hidden1(0, 0, pair_ps)
            graph_hidden1(0, 1, pair_ps)
            graph_head(1, early_ps)
            act.wait_ge(b1_loaded, DONE)
            run_steps(act, step)

        @block.tensor
        def _(pe):
            def three_passes(dst, w_hi, w_lo, v_hi, v_lo, start, stop):
                nc.tensor.matmul(dst, w_hi, v_hi, start=start, stop=False)
                nc.tensor.matmul(dst, w_hi, v_lo, start=False, stop=False)
                return nc.tensor.matmul(dst, w_lo, v_hi, start=False, stop=stop)

            def expert_up(m, parity, e, banks=hid_ps):
                if e == 0:
                    pe.wait_ge(xt_lo_ready, m + 1)
                if e >= len(banks) or isinstance(m, int) and m == GROUPS - 1:
                    pe.wait_ge(hid_ready, m * E + e + 1 - len(banks))
                three_passes(banks[e % len(banks)][:], up_hi[:, e, :], up_lo[:, e, :], xt_hi[parity][:],
                             xt_lo[parity][:], True, True).then_inc(hid_product, 1)

            def expert_down(m, e):
                if e in POOL_LOWS:
                    pe.wait_ge(gated_lo_pool_ready, m * len(POOL_LOWS) + POOL_LOWS.index(e) + 1)
                else:
                    pe.wait_ge(gated_lo_ready, lows_before(m, e))
                last = three_passes(yt_ps[:], down_hi[:, e, :], down_lo[:, e, :], gated_hi[e][:], gated_lo[e][:],
                                    False, e == E - 1)
                if e == E - 1:
                    last.then_inc(down_done, 1)

            def graph_ax(group, bank):
                pe.wait_ge(xhat1_done, group + 1)
                if not (isinstance(group, int) and group < 3):
                    pe.wait_ge(x1_done, group)
                for b in range(B):
                    last = nc.tensor.matmul(bank[:, b * P:(b + 1) * P], xhat1[:, b, :], a_t[:], start=True, stop=True)
                last.then_inc(ax_product, 1)

            def graph_hidden1(group, k, banks):
                if k == 0:
                    pe.wait_ge(ax_lo_ready, group + 1)
                for b in (2 * k, 2 * k + 1):
                    dst = banks[k][:, (b % 2) * H1:(b % 2 + 1) * H1]
                    hi, lo = ax_hi[:, b * P:(b + 1) * P], ax_lo[:, b * P:(b + 1) * P]
                    nc.tensor.matmul(dst, hi, w1_hi[:], start=True, stop=False)
                    nc.tensor.matmul(dst, hi, w1_lo[:], start=False, stop=False)
                    last = nc.tensor.matmul(dst, lo, w1_hi[:], start=False, stop=True)
                last.then_inc(h1_product, 1)

            def graph_ah(group):
                pe.wait_ge(h1_ready, group * 2 + 1)
                for k in range(C1):
                    for b in range(B):
                        if k == 0 and b == 2:
                            pe.wait_ge(h1_ready, group * 2 + 2)
                        last = nc.tensor.matmul(pair_ps[k][:, b * P:(b + 1) * P], h1[:, b, k * P:(k + 1) * P], a_t[:],
                                                start=True, stop=True)
                    last.then_inc(ah_product, 1)

            def graph_hidden2(s, j):
                if j == 0:
                    pe.wait_ge(ah_lo_ready, (s + 1) * C1)
                if j >= 2:
                    pe.wait_ge(h2_ready, s * C2 + j - 1)
                chunk = slice(j * P, (j + 1) * P)
                for k in range(C1):
                    last = three_passes(pair_ps[j % 2][:], w2_hi[:, k, chunk], w2_lo[:, k, chunk],
                                        ah_hi[:, k, :], ah_lo[:, k, :], k == 0, k == C1 - 1)
                last.then_inc(h2_product, 1)

            def graph_out(s, j):
                pe.wait_ge(h2_ready, s * C2 + j + 1)
                if j == 0 and ah_ahead(s):
                    pe.wait_ge(x1_done, s)
                for b in range(B):
                    last = nc.tensor.matmul(chain_ps[:, b * F:(b + 1) * F], h2_t[:, j, b * P:(b + 1) * P],
                                            w3_sb[:, j, :], start=(j == 0 and b == 0), stop=(j == C2 - 1),
                                            skip_group_check=True)
                return last

            def combine_across(c):
                pe.wait_ge(combine_done, c + 1)
                for b in range(B):
                    last = nc.tensor.transpose(route_ps[0:PARTS * E, b * P:(b + 1) * P],
                                               combine[:, b, :, :].rearrange("p k e -> p (k e)"), ident[:])
                last.then_inc(ct_product, 1)

            def turn(group):
                pe.wait_ge(xhat2_done, group + 1)
                for b in range(B):
                    last = nc.tensor.transpose(turn_ps[:, b * P:(b + 1) * P], xhat2[:, b, :], ident[:])
                last.then_inc(xt_product, 1)

            def route(group):
                pe.wait_ge(xt_ready, group + 1)
                if not (isinstance(group, int) and group == 0):
                    pe.wait_ge(ct_ready, group)
                for b in range(B):
                    last = nc.tensor.matmul(route_ps[:, b * E:(b + 1) * E], xt[:, b * P:(b + 1) * P], router[:],
                                            start=True, stop=True)
                last.then_inc(logits_product, 1)

            def expert_biases(m):
                pe.wait_ge(ct_ready, m + 1)
                nc.tensor.matmul(yt_ps[:], b2_parts[:], ct_parts[:], start=True, stop=False)

            def expert_sum(m, turned):
                pe.wait_ge(xt_lo_ready, turned)
                pe.wait_ge(yt_ready, m + 1)
                for b in range(B):
                    last = nc.tensor.transpose(turn_ps[:, b * F:(b + 1) * F], yt_sb[:, b * P:(b + 1) * P], ident[:])
                last.then_inc(y_product, 1)

            def step(s, parity, graph, next_group, load_ahead, select, experts):
                c, m = s - 1, s - 2
                if graph:
                    if not ah_ahead(s):
                        graph_ah(s)
                    if first_step(s):
                        graph_hidden1(1, 0, hid_ps)
                        graph_hidden1(1, 1, hid_ps)
                    if isinstance(s, int) and s == 2:
                        pe.wait_ge(b2_stacked, DONE)
                        pe.wait_ge(up_split, 1)
                        pe.wait_ge(down_split, 1)
                    if experts:
                        expert_up(m, parity, 0)
                        expert_up(m, parity, 1)
                        expert_biases(m)
                    if not turns_late(s):
                        pe.wait_ge(out_ready, s - 2)
                        turn(c)
                    graph_hidden2(s, 0)
                    if experts:
                        expert_up(m, parity, 2)
                        if turns_late(s):
                            expert_up(m, parity, 3)
                            turn(c)
                        else:
                            route(c)
                            expert_up(m, parity, 3)
                    for j in range(1, C2):
                        graph_hidden2(s, j)
                        if experts:
                            expert_up(m, parity, j + 3)
                        if select and turns_late(s):
                            if j == 1 and experts or j == 2 and not experts:
                                route(c)
                        graph_out(s, j - 1)
                        if select and not experts:
                            if j == 1:
                                turn(c)
                            if j == 3:
                                graph_ax(2, early_ps)
                    graph_out(s, C2 - 1).then_inc(s3_product, 1)
                    if experts:
                        expert_up(m, parity, 7)
                        combine_across(c)
                        expert_down(m, 0)
                    else:
                        if select:
                            graph_hidden1(2, 0, hid_ps)
                            graph_hidden1(2, 1, hid_ps)
                        graph_ah(s + 1)
                    if first_step(s):
                        pe.wait_ge(a_split, 1)
                    pe.wait_ge(s3_lo_ready, s + 1)
                    three_passes(chain_ps[:], a_hi[:], a_lo[:], s3_hi[:], s3_lo[:], True, True).then_inc(as3_product, 1)
                    if select and not experts:
                        combine_across(c)
                    if experts:
                        expert_down(m, 1)
                        expert_down(m, 2)
                    if next_group and experts:
                        graph_ax(s + 1, chain_ps)
                    if experts:
                        expert_down(m, 3)
                        expert_down(m, 4)
                        expert_down(m, 5)
                    if not next_group:
                        expert_up(m + 1, 1 - parity, 0, all_hid_ps)
                        turn(s)
                    if experts:
                        expert_down(m, 6)
                        expert_down(m, 7)
                    if next_group and experts:
                        graph_hidden1(s + 1, 0, pair_ps)
                        graph_hidden1(s + 1, 1, pair_ps)
                    elif not next_group:
                        route(s)
                    if experts:
                        expert_sum(m, s if next_group else s + 1)
                elif select:
                    expert_up(m, parity, 1, all_hid_ps)
                    expert_biases(m)
                    for e in range(2, E):
                        expert_up(m, parity, e, all_hid_ps)
                    for e in range(2):
                        expert_down(m, e)
                    for e in range(4):
                        expert_up(m + 1, 1 - parity, e, all_hid_ps)
                    combine_across(c)
                    for e in range(2, 4):
                        expert_down(m, e)
                    for e in range(4, 7):
                        expert_up(m + 1, 1 - parity, e, all_hid_ps)
                    for e in range(4, E):
                        expert_down(m, e)
                    expert_up(m + 1, 1 - parity, 7, all_hid_ps)
                    expert_sum(m, s)
                else:
                    pe.wait_ge(ct_ready, m + 1)
                    for b in range(B):
                        nc.tensor.matmul(final_ps[:, b * F:(b + 1) * F], ct_parts[:, b * P:(b + 1) * P], b2_parts[:],
                                         start=b == 0, stop=False, skip_group_check=True)
                    for e in range(E):
                        pe.wait_ge(gated_ready, m * E + e + 1)
                        for b in range(B):
                            tokens = slice(b * P, (b + 1) * P)
                            last = nc.tensor.matmul(final_ps[:, b * F:(b + 1) * F], gated[e % GATED_BUFS][:, tokens],
                                                    down_raw[:, e, :], start=False, stop=e == E - 1,
                                                    skip_group_check=True)
                        last.then_inc(final_down if e < E - 1 else y_product, 1)

            pe.wait_ge(consts_ready, 1)
            for _ in range(WAKING):
                nc.tensor.matmul(turn_ps[:, 0:P], ident[:], ident[:], start=True, stop=True)
            pe.wait_ge(a_ready, 1)
            graph_ax(0, chain_ps)
            pe.wait_ge(w1_split, 1)
            graph_hidden1(0, 0, pair_ps)
            graph_hidden1(0, 1, pair_ps)
            graph_ax(1, early_ps)
            pe.wait_ge(w2_split, 1)
            pe.wait_ge(w3_loaded, DONE)
            pe.wait_ge(router_loaded, DONE)
            run_steps(pe, step)


_OUT = "out_dram"


def kernel(x, adj, L0_gnn_W1, L0_gnn_W2, L0_gnn_W3, L0_ffn_router_w, L0_ffn_w1, L0_ffn_b1, L0_ffn_w2, L0_ffn_b2):
    import numpy as np
    import concourse.bacc as bacc
    from concourse import mybir as mb
    from concourse.bass_utils import run_bass_kernel_spmd

    batches, nodes, features = x.shape
    per_group = 4
    groups = batches // per_group

    def grouped(a):
        return a.reshape(groups, per_group, nodes, features).transpose(0, 2, 1, 3).reshape(groups, nodes, -1)

    laid_out = {
        "x": grouped(np.asarray(x)),
        "adj_t": np.asarray(adj).T,
        "gnn_w1": np.asarray(L0_gnn_W1),
        "gnn_w2": np.asarray(L0_gnn_W2),
        "gnn_w3": np.asarray(L0_gnn_W3),
        "router_t": np.asarray(L0_ffn_router_w).T,
        "ffn_w1": np.asarray(L0_ffn_w1).transpose(1, 0, 2),
        "ffn_b1_t": np.asarray(L0_ffn_b1).T,
        "ffn_w2": np.asarray(L0_ffn_w2).transpose(1, 0, 2),
        "ffn_b2": np.asarray(L0_ffn_b2),
    }
    nc = bacc.Bacc("TRN2", target_bir_lowering=False, num_devices=1)
    arrays, args = {}, []
    for name, a in laid_out.items():
        a = np.ascontiguousarray(a)
        arrays[f"in_{name}"] = a
        args.append(nc.dram_tensor(f"in_{name}", a.shape, mb.dt.from_np(a.dtype), kind="ExternalInput").ap())
    out = nc.dram_tensor(_OUT, (groups, nodes, per_group * features), mb.dt.float32, kind="ExternalOutput").ap()
    gnn_moe_kernel(nc, *args, out)
    result = run_bass_kernel_spmd(nc, [arrays], core_ids=[0]).results[0][_OUT]
    return (result.reshape(groups, nodes, per_group, features).transpose(0, 2, 1, 3)
            .reshape(batches, nodes, features))
```
